# Optimizing a Trainium2 kernel written in Bass

```python
import numpy as np
import jax
import jax.numpy as jnp

def _softmax(x, axis=-1):
    return jax.nn.softmax(x, axis=axis)

def _gelu(x):
    return jax.nn.gelu(x, approximate=True)

def _silu(x):
    return jax.nn.silu(x)

def _sigmoid(x):
    return jax.nn.sigmoid(x)

def _layernorm(x, axis=-1, eps=1e-05):
    m = jnp.mean(x, axis=axis, keepdims=True)
    v = jnp.var(x, axis=axis, keepdims=True)
    return (x - m) / jnp.sqrt(v + eps)

def _scatter_add(tgt, idx, src, axis=0):
    return tgt.at[idx].add(src)

def _segment_sum(src, seg, n):
    return jax.ops.segment_sum(src, seg, n)
kernel_name = 'mk_vit_tower_postln_d1_tok_img768_r4_eac02f'

def setup_inputs(seed: int=0):
    np.random.seed(seed)
    _w = jnp.asarray

    def _rec_inputs():
        import jax
        import jax.numpy as jnp
        _rk = jax.random.key(seed)
        x = -0.00016672 + 0.999947 * jax.random.normal(jax.random.fold_in(_rk, 1), (16, 96, 96, 3), jnp.float32)
        return x
    x = _rec_inputs()

    def _L0_tok_setup():
        import jax, jax.numpy as jnp
        import numpy as np
        PATCH = 16
        D_MODEL = 192

        def _patchify(imgs, p):
            B, H, Wd, C = imgs.shape
            nh, nw = (H // p, Wd // p)
            x = imgs.reshape(B, nh, p, nw, p, C)
            x = x.transpose(0, 1, 3, 2, 4, 5)
            return x.reshape(B, nh * nw, p * p * C)
        key = jax.random.key(seed)
        k1, k2 = jax.random.split(key)
        B, H, W_, C = (64, 96, 96, 3)
        imgs = jax.random.normal(k1, (B, H, W_, C), dtype=jnp.float32)
        patch_dim = PATCH * PATCH * C
        W = jax.random.normal(k2, (patch_dim, D_MODEL), dtype=jnp.float32) * (1.0 / np.sqrt(patch_dim))
        b = jnp.zeros((D_MODEL,), dtype=jnp.float32)
        return {'imgs': imgs, 'W': W, 'b': b}
    _L0_tok_all = _L0_tok_setup()
    _L0_tok_in = {k: v for k, v in _L0_tok_all.items() if k in ('W', 'b')}
    del _L0_tok_all

    def _L0_attn_setup():
        import jax, jax.numpy as jnp
        import numpy as np
        DIM = 192
        HEADS = 12
        DIM_HEAD = 64
        INNER = HEADS * DIM_HEAD
        L = 64
        EPS = 1e-08
        key = jax.random.key(seed)
        k1, k2, k3, k4 = jax.random.split(key, 4)
        x = jax.random.normal(k1, (2, 1024, DIM), dtype=jnp.float32)
        w_qkv = jax.random.normal(k2, (3 * INNER, DIM), dtype=jnp.float32) * DIM ** (-0.5)
        w_out = jax.random.normal(k3, (DIM, INNER), dtype=jnp.float32) * INNER ** (-0.5)
        b_out = jax.random.normal(k4, (DIM,), dtype=jnp.float32) * 0.01
        scale = jnp.full((HEADS,), np.log2(L * L - L), dtype=jnp.float32)
        return {'x': x, 'w_qkv': w_qkv, 'w_out': w_out, 'b_out': b_out, 'scale': scale}
    _L0_attn_all = _L0_attn_setup()
    _L0_attn_in = {k: v for k, v in _L0_attn_all.items() if k in ('w_qkv', 'w_out', 'b_out', 'scale')}
    del _L0_attn_all

    def _L0_ffn_setup():
        import jax, jax.numpy as jnp
        import numpy as np
        ALPHA = 1.702
        LIMIT = 7.0
        TOP_K = 2
        B, S, H, E, I = (2, 256, 192, 8, 192)
        key = jax.random.key(seed)
        ks = jax.random.split(key, 7)
        scale = 0.02
        return {'hidden_states': jax.random.normal(ks[0], (B, S, H), dtype=jnp.float32), 'Wr': jax.random.normal(ks[1], (H, E), dtype=jnp.float32) * scale, 'br': jax.random.normal(ks[2], (E,), dtype=jnp.float32) * scale, 'Wgu': jax.random.normal(ks[3], (E, H, 2 * I), dtype=jnp.float32) * scale, 'bgu': jax.random.normal(ks[4], (E, 2 * I), dtype=jnp.float32) * scale, 'Wd': jax.random.normal(ks[5], (E, I, H), dtype=jnp.float32) * scale, 'bd': jax.random.normal(ks[6], (E, H), dtype=jnp.float32) * scale}
    _L0_ffn_all = _L0_ffn_setup()
    _L0_ffn_in = {k: v for k, v in _L0_ffn_all.items() if k in ('Wr', 'br', 'Wgu', 'bgu', 'Wd', 'bd')}
    del _L0_ffn_all
    return {'x': x, 'L0_tok_W': _L0_tok_in['W'], 'L0_tok_b': _L0_tok_in['b'], 'L0_attn_w_qkv': _L0_attn_in['w_qkv'], 'L0_attn_w_out': _L0_attn_in['w_out'], 'L0_attn_b_out': _L0_attn_in['b_out'], 'L0_attn_scale': _L0_attn_in['scale'], 'L0_ffn_Wr': _L0_ffn_in['Wr'], 'L0_ffn_br': _L0_ffn_in['br'], 'L0_ffn_Wgu': _L0_ffn_in['Wgu'], 'L0_ffn_bgu': _L0_ffn_in['bgu'], 'L0_ffn_Wd': _L0_ffn_in['Wd'], 'L0_ffn_bd': _L0_ffn_in['bd']}

def reference(x, L0_tok_W, L0_tok_b, L0_attn_w_qkv, L0_attn_w_out, L0_attn_b_out, L0_attn_scale, L0_ffn_Wr, L0_ffn_br, L0_ffn_Wgu, L0_ffn_bgu, L0_ffn_Wd, L0_ffn_bd):
    import jax
    import jax.numpy as jnp

    def _L0_tok_ref(imgs, W, b):
        import jax, jax.numpy as jnp
        import numpy as np
        PATCH = 16
        D_MODEL = 192

        def _patchify(imgs, p):
            B, H, Wd, C = imgs.shape
            nh, nw = (H // p, Wd // p)
            x = imgs.reshape(B, nh, p, nw, p, C)
            x = x.transpose(0, 1, 3, 2, 4, 5)
            return x.reshape(B, nh * nw, p * p * C)
        x = _patchify(imgs, PATCH)
        return jnp.einsum('bnd,de->bne', x, W) + b

    def _L0_attn_ref(x, w_qkv, w_out, b_out, scale):
        import jax, jax.numpy as jnp
        import numpy as np
        DIM = 192
        HEADS = 12
        DIM_HEAD = 64
        INNER = HEADS * DIM_HEAD
        L = 64
        EPS = 1e-08
        b, n, d = x.shape
        h, dh = (HEADS, DIM_HEAD)
        qkv = x @ w_qkv.T
        q, k, v = jnp.split(qkv, 3, axis=-1)
        q, k, v = (t.reshape(b, n, h, dh).transpose(0, 2, 1, 3) for t in (q, k, v))
        q = q * jax.lax.rsqrt(jnp.linalg.norm(q, axis=1, keepdims=True) + EPS)
        k = k * jax.lax.rsqrt(jnp.linalg.norm(k, axis=1, keepdims=True) + EPS)
        dots = jnp.einsum('bhid,bhjd->bhij', q, k)
        scores = jax.nn.softmax(dots / scale[:, None, None], axis=-1)
        out = jnp.einsum('bhij,bhjd->bhid', scores, v)
        out = out.transpose(0, 2, 1, 3).reshape(b, n, h * dh)
        return out @ w_out.T + b_out

    def _L0_ffn_ref(hidden_states, Wr, br, Wgu, bgu, Wd, bd):
        import jax, jax.numpy as jnp
        import numpy as np
        ALPHA = 1.702
        LIMIT = 7.0
        TOP_K = 2
        B, S, H, E, I = (2, 256, 192, 8, 192)
        logits = jnp.einsum('bsh,he->bse', hidden_states, Wr) + br
        topk_vals, topk_idx = jax.lax.top_k(logits, TOP_K)
        router_scores = jax.nn.softmax(topk_vals, axis=-1)
        gu = jnp.einsum('bsh,ehf->bsef', hidden_states, Wgu) + bgu
        gu = jnp.minimum(gu, LIMIT)
        gate = gu[..., :I]
        up = jnp.maximum(gu[..., I:], -LIMIT)
        glu = gate * jax.nn.sigmoid(gate * ALPHA)
        activated = (up + 1.0) * glu
        down = jnp.einsum('bsei,eih->bseh', activated, Wd) + bd
        sel = jnp.take_along_axis(down, topk_idx[..., None], axis=2)
        output = jnp.sum(sel * router_scores[..., None], axis=2)
        return output
    h = _L0_tok_ref(x, L0_tok_W, L0_tok_b)
    h = _layernorm(h + _L0_attn_ref(h, L0_attn_w_qkv, L0_attn_w_out, L0_attn_b_out, L0_attn_scale), axis=-1)
    h = _layernorm(h + _L0_ffn_ref(h, L0_ffn_Wr, L0_ffn_br, L0_ffn_Wgu, L0_ffn_bgu, L0_ffn_Wd, L0_ffn_bd), axis=-1)
    return h

_drawn_inputs = setup_inputs


def setup_inputs(seed=0):
    import zlib

    import numpy as np

    out = dict(_drawn_inputs(seed))
    spreads = {'L0_tok_b': (0.0, 0.1), 'L0_attn_scale': (11.977279663085938, 0.6)}
    factors = {'L0_attn_b_out': 5.87, 'L0_ffn_br': 8.0, 'L0_ffn_bgu': 23.885, 'L0_ffn_bd': 3.932}
    for name, (base, spread) in spreads.items():
        noise = np.random.default_rng([zlib.crc32(name.encode()), seed]).standard_normal(out[name].shape)
        drawn = base * np.exp(spread * noise) if base else spread * noise
        out[name] = jnp.asarray(drawn.astype(out[name].dtype))
    for name, factor in factors.items():
        out[name] = (out[name] * factor).astype(out[name].dtype)
    return out
```

```python
import concourse.bass as bass
from concourse import mybir
from contextlib import ExitStack


D = 192
DA, DB = 128, 64
PD, NC = 768, 6
B, SEQ = 16, 36
T = B * SEQ
TH = T // 2
H, DH = 12, 64
NP = H // 2
E, FI = 8, 192
NPAIR = E // 2
NT = 3 * NPAIR
IMG = 3
GRP = IMG * SEQ
SIZES = [GRP] * (B // IMG) + [SEQ * (B % IMG)] * (B % IMG > 0)
OFFS = [GRP * g for g in range(len(SIZES))]
NG = len(SIZES)
BANK = 512
HB = 4
NB = H // HB
LN_EPS, NORM_EPS = 1e-5, 1e-8
ALPHA, LIMIT = 1.702, 7.0
MASKED = -2.0 ** 126

C_TOKB, C_SCALE, C_BR, C_BGU, C_IOTA, C_BOUT, C_WR, C_BD = 0, 2, 8, 16, 40, 48, 240, 256
C_SMALL = C_BD + D

STG = 3
STGW = 1152
XW = T + 2 * 128
XR = 3


def vit_layer(nc, xT, w_tok, w_qkv_a, w_qkv_b, w_out, w_gu_a, w_gu_b, w_down, small, out):
    f32, f32r, bf16, u32 = mybir.dt.float32, mybir.dt.float32r, mybir.dt.bfloat16, mybir.dt.uint32
    ALU = mybir.AluOpType
    ACT = mybir.ActivationFunctionType
    X = mybir.AxisListType.X

    ctx = ExitStack()
    with ctx:
        def sb(name, shape, dt=f32):
            return ctx.enter_context(nc.sbuf_tensor(name, shape, dt))

        def sem(name):
            return ctx.enter_context(nc.semaphore(name))

        def f(ap):
            return ap.bitcast(f32)

        reg_a = sb("reg_a", [128, 15696], f32r)
        reg_b = sb("reg_b", [128, 12288], f32r)
        reg_c = sb("reg_c", [128, 5328], f32r)
        h1T = sb("h1T", [128, 3, T], f32r)
        w2T = sb("w2T", [40, T], f32r)
        onehot = sb("onehot", [40, E, 128], f32r)
        ident_r = sb("ident_r", [128, 128], f32r)
        fold_r = sb("fold_r", [128, 128], f32r)
        small_hi = sb("small_hi", [128, 16 + D], f32r)
        small_lo = sb("small_lo", [128, 16 + D], f32r)
        mask_l = sb("mask_l", [128, GRP], bf16)
        mask_r = sb("mask_r", [128, HB * GRP], bf16)

        xw = reg_a[:, 0:XR * 2 * XW].rearrange("p (s k n) -> p s k n", s=XR, k=2)
        V = reg_a[:, 0:NG * 2 * PD].rearrange("p (g k n) -> p g k n", g=NG, k=2)
        Q = reg_a[:, 9216:9216 + 2 * NP * GRP].rearrange("p (k m n) -> p k m n", k=2, m=NP)
        K = reg_a[:, 10512:10512 + 4 * NP * GRP].rearrange("p (k m a n) -> p k m a n", k=2, m=NP, a=2)
        PT = reg_a[:, 13104:13104 + 2 * H * GRP].rearrange("p (k n) -> p k n", k=2)
        acts = reg_a[:, 0:2 * NT * T].rearrange("p (c k n) -> p c k n", c=NT, k=2)
        wqkv = reg_b[:, 0:4 * 3 * PD].rearrange("p (s c k n) -> p s c k n", s=3, c=2, k=2)
        wgu = reg_b[:, :].rearrange("p (s c k n) -> p s c k n", s=NPAIR, c=2, k=2)
        wout = reg_c[:, 0:2 * NC * D].rearrange("p (k c n) -> p k c n", k=2, c=NC)
        hT = reg_c[:, 2304:2304 + 3 * T].rearrange("p (k n) -> p k n", k=3)
        oT = reg_c[:, 4032:4032 + 2 * NP * GRP].rearrange("p (k m n) -> p k m n", k=2, m=NP)
        wd = reg_c[:, 0:4 * STGW].rearrange("p (s k n) -> p s k n", s=2, k=2)

        stage = sb("stage", [128, STG, STGW])
        reg_q = sb("reg_q", [128, 12 * T])
        qk_raw = reg_q[:, :].rearrange("p (m n) -> p m n", m=12)
        tmp = reg_q[:, :].rearrange("p (s k n) -> p s k n", s=2, k=6)
        rnorm = sb("rnorm", [128, 2, T])
        Pr = sb("Pr", [128, H * GRP])
        h1 = sb("h1", [128, NG, 256])
        sq = Pr[:, 0:2 * T].rearrange("p (k n) -> p k n", k=2)
        ss = h1[:, :, :].rearrange("p g n -> p (g n)")[:, 0:2 * T].rearrange("p (k n) -> p k n", k=2)
        ss_r = reg_a[:, 13104:13104 + 4 * T].rearrange("p (t k n) -> p t k n", t=2, k=2)
        sm = sb("sm", [128, C_SMALL])
        inv_scale = sb("inv_scale", [128, NP])
        bup1 = sb("bup1", [128, NT])
        small_eps = sb("small_eps", [128, 1])
        ident = sb("ident", [128, 128])
        half = sb("half", [128, 1])
        negm = sb("negm", [128, H])
        mx = sb("mx", [128, H])
        psum_e = sb("psum_e", [128, H])
        rinv = sb("rinv", [128, H])
        y = sb("y", [128, D])
        stats = sb("stats", [128, 6])
        mv = sb("mv", [128, 2])
        var_e = sb("var_e", [128, 1])
        rstd = sb("rstd", [128, 1])
        lg = sb("lg", [128, 8])
        top = sb("top", [128, 8])
        top_i = sb("top_i", [128, 8], u32)
        rt = sb("rt", [128, 8])
        sel = sb("sel", [128, 2, 8])
        w2 = sb("w2", [128, 40])
        z = rnorm[:, 0, 0:2 * D].rearrange("p (k n) -> p k n", k=2)
        res = rnorm[:, 1, 0:2 * D].rearrange("p (k n) -> p k n", k=2)
        onehot_f = Pr[0:40, 0:E * 128].rearrange("p (e n) -> p e n", e=E)
        fold_f = rnorm[:, 0, 0:128]
        mask_lf = rnorm[:, 0, 128:128 + GRP]
        mask_rf = rnorm[:, 1, 0:HB * GRP]

        ps = ctx.enter_context(nc.psum_tensor("ps", [128, 8, BANK], f32))

        def halves(bank):
            return ps[:, bank:bank + 2, 0:TH]

        def two(ap):
            return ap.rearrange("p (a n) -> p a n", a=2)

        s_stage = [sem(f"s_stage{i}") for i in range(STG)]
        s_small = sem("s_small")
        s_out = [sem(f"s_out{i}") for i in range(2)]
        (s_fill, s_sel, s_const, s_smprep, s_smhi, s_smlo, s_xhi, s_xlo, s_whi, s_wlo, s_tok, s_hthi, s_htlo,
         s_qk, s_raw, s_sq, s_ssq, s_ssk, s_sshi, s_sslo, s_nsum, s_nsqrt, s_nln, s_r, s_v, s_vhi, s_vlo,
         s_qn, s_kn, s_qhi, s_qlo, s_khi, s_klo, s_s, s_mx, s_negm, s_e, s_rinv, s_p, s_pt, s_pthi, s_ptlo, s_pv,
         s_ohi, s_olo, s_op, s_y, s_st, s_mv, s_ve, s_rstd, s_h1, s_ht1, s_h1hi, s_h1lo, s_rt, s_lg, s_top, s_ti,
         s_gap, s_egap, s_rs, s_p1, s_p2, s_sel2, s_w2, s_wt, s_wthi, s_wtlo, s_gu, s_g, s_sig, s_glu, s_wbc,
         s_glw, s_u, s_act, s_ahi, s_alo, s_dn, s_z, s_zst, s_zmv, s_zve, s_zrstd, s_res) = [
            sem(n) for n in (
                "s_fill s_sel s_const s_smprep s_smhi s_smlo s_xhi s_xlo s_whi s_wlo s_tok s_hthi s_htlo "
                "s_qk s_raw s_sq s_ssq s_ssk s_sshi s_sslo s_nsum s_nsqrt s_nln s_r s_v s_vhi s_vlo "
                "s_qn s_kn s_qhi s_qlo s_khi s_klo s_s s_mx s_negm s_e s_rinv s_p s_pt s_pthi s_ptlo s_pv "
                "s_ohi s_olo s_op s_y s_st s_mv s_ve s_rstd s_h1 s_ht1 s_h1hi s_h1lo s_rt s_lg s_top s_ti "
                "s_gap s_egap s_rs s_p1 s_p2 s_sel2 s_w2 s_wt s_wthi s_wtlo s_gu s_g s_sig s_glu s_wbc "
                "s_glw s_u s_act s_ahi s_alo s_dn s_z s_zst s_zmv s_zve s_zrstd s_res").split()]

        pieces = []
        for c in range(NC):
            pieces.append(([(xT[c], 0, 128, 0, T), (w_tok[c], 0, 128, T, 256)], XW, xw[:, c % XR]))
        for s in range(3):
            pieces.append(([(w_qkv_a[s], 0, 128, 0, PD)], PD, wqkv[:, s, 0]))
            pieces.append(([(w_qkv_b[s], 0, 64, 0, PD), (w_qkv_b[s], 64, 128, 0, PD)], PD, wqkv[:, s, 1]))
        pieces.append(([(w_out, 0, 128, 0, NC * D)], NC * D, wout.rearrange("p k c n -> p k (c n)")))
        for s in range(NPAIR):
            pieces.append(([(w_gu_a[s], 0, 128, 0, 768)], 768, wgu[:, s, 0]))
            pieces.append(([(w_gu_b[s], 0, 64, 0, 768), (w_gu_b[s], 64, 128, 0, 768)], 768, wgu[:, s, 1]))
        for s in range(2):
            pieces.append(([(w_down[s], 0, 128, 0, STGW)], STGW, wd[:, s]))
        P_QKV, P_OUT, P_GU = NC, NC + 6, NC + 7
        P_DN = P_GU + 2 * NPAIR
        arrived = []
        for k, (loads, _, _) in enumerate(pieces):
            arrived.append(16 * len(loads) + (arrived[k - STG] if k >= STG else 0))

        def w_ready(k):
            return k - NC + 1

        block = ctx.enter_context(nc.Block())

        @block.sync
        def _(sp):
            for k, (loads, _, _) in enumerate(pieces):
                if k - STG >= NC:
                    sp.wait_ge(s_wlo, w_ready(k - STG))
                elif k >= STG:
                    sp.wait_ge(s_xlo, k - STG + 1)
                for src, p0, p1, c0, n in loads:
                    sp.dma_start(stage[p0:p1, k % STG, c0:c0 + n], src).then_inc(s_stage[k % STG], 16)
                if k == 0:
                    sp.dma_start(sm[:, :], small).then_inc(s_small, 16)
            for g in range(NG):
                sp.wait_ge(s_res, g + 1)
                sp.dma_start(out[OFFS[g]:OFFS[g] + SIZES[g], :], res[0:SIZES[g], g % 2, :])\
                    .then_inc(s_out[g % 2], 16)
            for i in range(2):
                sp.wait_ge(s_out[i], 16 * (NG // 2))

        @block.gpsimd
        def _(pool):
            for t in (ident[:, :], fold_f, onehot_f, mask_lf, half[:, :]):
                nc.gpsimd.memset(t, -0.5 if t.shape[-1] == 1 else 0.0).then_inc(s_fill, 1)
            nc.gpsimd.memset(mask_rf, MASKED).then_inc(s_fill, 1)
            pool.wait_ge(s_fill, 6)
            nc.gpsimd.memset(f(K[64:128, :, :, 0]), 0.0).then_inc(s_fill, 1)
            pool.wait_ge(s_fill, 7)
            nc.gpsimd.memset(f(K[0:64, :, :, 1]), 0.0).then_inc(s_fill, 1)
            pool.wait_ge(s_fill, 8)

            def fill(ap, base, pattern, value, n):
                pool.wait_ge(s_sel, n)
                nc.gpsimd.affine_select(out=ap, in_=ap, compare_op=ALU.not_equal, fill=value, base=base,
                                        pattern=pattern, channel_multiplier=1).then_inc(s_sel, 1)
            nc.gpsimd.affine_select(out=ident[:, :], in_=ident[:, :], compare_op=ALU.not_equal, fill=1.0, base=0,
                                    pattern=[[-1, 128]], channel_multiplier=1).then_inc(s_sel, 1)
            fold3 = fold_f.rearrange("p (a n) -> p a n", a=2)
            fill(fold3, 0, [[0, 2], [-1, 64]], 1.0, 1)
            fill(fold3, -64, [[0, 2], [-1, 64]], 1.0, 2)
            fill(mask_lf.rearrange("p (a n) -> p a n", a=IMG), 0, [[-1, IMG], [0, SEQ]], 1.0, 3)
            fill(mask_rf.rearrange("p (h a n) -> p h a n", h=HB, a=IMG), 0, [[0, HB], [-1, IMG], [0, SEQ]], 0.0, 4)
            fill(onehot_f, 0, [[-1, E], [0, 128]], 1.0, 5)
            fill(onehot_f, -32, [[-1, E], [0, 128]], 1.0, 6)

            def w_lo(k):
                _, n, dst = pieces[k]
                pool.wait_ge(s_stage[k % STG], arrived[k])
                pool.wait_ge(s_whi, w_ready(k))
                if P_GU <= k:
                    pool.wait_ge(s_v, NG)
                if P_DN <= k:
                    pool.wait_ge(s_op, NG)
                nc.gpsimd.tensor_tensor(dst[:, 1, :], stage[:, k % STG, 0:n], f(dst[:, 0, :]),
                                        ALU.subtract).then_inc(s_wlo, 1)
            for k in range(P_QKV, P_QKV + 4):
                w_lo(k)
            for m in range(7, 12):
                pool.wait_ge(s_sq, m + 1)
                if m > 7:
                    pool.wait_ge(s_ssk, m - 7)
                nc.gpsimd.tensor_tensor(ss[:, 1], ss[:, 1], sq[:, m % 2], ALU.add).then_inc(s_ssk, 1)
                if m == 7:
                    w_lo(P_QKV + 4)
                    w_lo(P_QKV + 5)
            w_lo(P_OUT)
            w_at = P_GU

            def k_norm(g):
                n, o = SIZES[g], OFFS[g]
                kk = qk_raw[:, NP:2 * NP, o:o + n]
                if g == 0:
                    pool.wait_ge(s_r, 2)
                    pool.wait_ge(s_raw, 12)
                nc.gpsimd.tensor_tensor(kk, kk, rnorm[:, 1:2, o:o + n].to_broadcast([128, NP, n]),
                                        ALU.mult).then_inc(s_kn, 1)

            def k_lo(g):
                n, o = SIZES[g], OFFS[g]
                pool.wait_ge(s_kn, g + 1)
                pool.wait_ge(s_khi, 2 * (g + 1))
                if g >= 1:
                    pool.wait_ge(s_s, g)
                for a in range(2):
                    r = slice(64 * a, 64 * a + 64)
                    if a == 1:
                        pool.wait_ge(s_klo, 2 * g + 1)
                    nc.gpsimd.tensor_tensor(K[r, 1, :, a, 0:n], qk_raw[r, NP:2 * NP, o:o + n], f(K[r, 0, :, a, 0:n]),
                                            ALU.subtract).then_inc(s_klo, 1)
                pool.wait_ge(s_klo, 2 * g + 2)

            def probs(g):
                n = SIZES[g]
                pool.wait_ge(s_rinv, g + 1)
                pool.wait_ge(s_e, H * (g + 1))
                pp = Pr[0:n, 0:H * n].rearrange("p (h j) -> p h j", h=H)
                nc.gpsimd.tensor_tensor(pp, pp, rinv[0:n, :].unsqueeze(2).to_broadcast([n, H, n]),
                                        ALU.mult).then_inc(s_p, 1)

            def root(g, ve, done):
                n = SIZES[g]
                pool.wait_ge(ve, g + 1)
                nc.gpsimd.tensor_tensor(rstd[0:n, :], var_e[0:n, :], half[0:n, :], ALU.pow).then_inc(done, 1)

            k_norm(0)
            k_lo(0)
            w_at = P_GU
            for i in range(NG + 2):
                if 1 <= i <= NG:
                    probs(i - 1)
                if i + 1 < NG:
                    k_norm(i + 1)
                    k_lo(i + 1)
                if 2 <= i:
                    root(i - 2, s_ve, s_rstd)
                for _ in range(2):
                    if w_at < P_DN:
                        w_lo(w_at)
                        w_at += 1
            while w_at < P_DN + 2:
                w_lo(w_at)
                w_at += 1
            for c in range(NT):
                t = tmp[:, c % 2]
                pool.wait_ge(s_g, c + 1)
                pool.wait_ge(s_sig, c + 1)
                nc.gpsimd.tensor_tensor(t[:, 1], t[:, 0], t[:, 1], ALU.mult).then_inc(s_glu, 1)
                pool.wait_ge(s_wbc, c + 1)
                pool.wait_ge(s_glu, c + 1)
                nc.gpsimd.tensor_tensor(t[:, 1], t[:, 1], t[:, 2], ALU.mult).then_inc(s_glw, 1)
            for g in range(NG):
                root(g, s_zve, s_zrstd)

        @block.scalar
        def _(act):
            def w_hi(k):
                _, n, dst = pieces[k]
                act.wait_ge(s_stage[k % STG], arrived[k])
                if k < NC:
                    if k >= XR:
                        act.wait_ge(s_tok, k - XR + 1)
                elif k >= P_DN:
                    act.wait_ge(s_op, NG)
                elif k >= P_GU:
                    act.wait_ge(s_v, NG)
                nc.scalar.activation(dst[:, 0, :], stage[:, k % STG, 0:n], ACT.Copy)\
                    .then_inc(s_xhi if k < NC else s_whi, 1)
            w_hi(0)
            act.wait_ge(s_small, 16)
            nc.scalar.activation(small_hi[:, :], sm[:, C_WR:C_SMALL], ACT.Copy).then_inc(s_smhi, 1)
            for c in range(1, NC):
                w_hi(c)
            for k in range(P_QKV, P_QKV + 4):
                w_hi(k)
            act.wait_ge(s_tok, NC)
            for t in range(2):
                nc.scalar.activation(two(hT[:, t]), halves(4 + 2 * t), ACT.Identity,
                                     bias=sm[:, C_TOKB + t:C_TOKB + t + 1]).then_inc(s_hthi, 1)
            w_hi(P_QKV + 4)
            w_hi(P_QKV + 5)

            def root(t):
                act.wait_ge(s_nsum, t + 1)
                nc.scalar.activation(two(rnorm[:, t]), halves(4 + 2 * t), ACT.Sqrt).then_inc(s_nsqrt, 1)

            def ss_hi(t):
                act.wait_ge(s_ssk if t else s_ssq, 5)
                nc.scalar.activation(ss_r[:, t, 0], ss[:, t], ACT.Copy).then_inc(s_sshi, 1)

            act.wait_ge(s_const, 1)
            for m in range(12):
                if m == 8:
                    ss_hi(0)
                act.wait_ge(s_qk, m + 1)
                if m % 6 >= 3:
                    act.wait_ge(s_ssk if m >= 6 else s_ssq, m % 6 - 2)
                dst = ss[:, m // 6] if m % 6 == 0 else sq[:, m % 2]
                if m in (7, 8):
                    act.wait_ge(s_ssq, 5)
                nc.scalar.activation(two(dst), halves(2 * (m % 2)), ACT.Square).then_inc(s_sq, 1)
            w_hi(P_OUT)
            root(0)

            def v_hi(g):
                n = SIZES[g]
                act.wait_ge(s_v, g + 1)
                nc.scalar.activation(V[0:n, g, 0].rearrange("p (a n) -> p a n", a=2),
                                     ps[0:n, 0 + 2 * (g % 2):2 + 2 * (g % 2), 0:PD // 2], ACT.Copy).then_inc(s_vhi, 1)
            ss_hi(1)
            v_hi(0)
            root(1)
            v_hi(1)
            for t in range(2):
                act.wait_ge(s_nsqrt, t + 1)
                nc.scalar.activation(rnorm[:, t], rnorm[:, t], ACT.Ln, bias=small_eps[:, :]).then_inc(s_nln, 1)
            for t in range(2):
                act.wait_ge(s_nln, t + 1)
                nc.scalar.activation(rnorm[:, t], rnorm[:, t], ACT.Exp, scale=-0.5).then_inc(s_r, 1)
            for g in range(2, NG):
                v_hi(g)

            def k_hi(g):
                n, o = SIZES[g], OFFS[g]
                act.wait_ge(s_kn, g + 1)
                if g >= 1:
                    act.wait_ge(s_s, g)
                for a in range(2):
                    r = slice(64 * a, 64 * a + 64)
                    nc.scalar.activation(K[r, 0, :, a, 0:n], qk_raw[r, NP:2 * NP, o:o + n], ACT.Copy).then_inc(s_khi, 1)

            def o_hi(g):
                n = SIZES[g]
                act.wait_ge(s_pv, g + 1)
                if g >= 1:
                    act.wait_ge(s_op, g)
                for a in range(2):
                    nc.scalar.activation(oT[64 * a:64 * a + 64, 0, :, 0:n].rearrange("p (b m) n -> p b m n", b=NB),
                                         ps[64 * a:64 * a + 64, 3:6, 0:HB * n].rearrange(
                                             "p b (m a n) -> p b m a n", m=2, a=2)[:, :, :, a], ACT.Copy)\
                        .then_inc(s_ohi, 1)

            def pt_hi(g):
                n = SIZES[g]
                act.wait_ge(s_pt, g + 1)
                if g >= 1:
                    act.wait_ge(s_pv, g)
                for b in range(NB):
                    nc.scalar.activation(PT[0:n, 0, b * HB * n:(b + 1) * HB * n], ps[0:n, 3 + b, 0:HB * n],
                                         ACT.Copy).then_inc(s_pthi, 1)

            def h1_hi(g):
                n, o = SIZES[g], OFFS[g]
                act.wait_ge(s_ht1, g + 1)
                nc.scalar.activation(h1T[:, 0:2, o:o + n], ps[:, 7, 0:2 * n].rearrange("p (k n) -> p k n", k=2),
                                     ACT.Copy).then_inc(s_h1hi, 1)

            def exps(g):
                n = SIZES[g]
                act.wait_ge(s_negm, g + 1)
                if g >= 1:
                    act.wait_ge(s_pt, g)
                    act.wait_ge(s_rinv, g)
                for h in range(H):
                    nc.scalar.activation(Pr[0:n, h * n:(h + 1) * n], ps[0:n, h // HB, (h % HB) * n:(h % HB + 1) * n],
                                         ACT.Exp, bias=negm[0:n, h:h + 1], accum_out=psum_e[0:n, h:h + 1])\
                        .then_inc(s_e, 1)

            def gap_exp(g):
                n = SIZES[g]
                act.wait_ge(s_gap, g + 1)
                nc.scalar.activation(rt[0:n, 3:4], rt[0:n, 2:3], ACT.Exp).then_inc(s_egap, 1)

            def w_hi_t(g):
                n, o = SIZES[g], OFFS[g]
                act.wait_ge(s_wt, g + 1)
                nc.scalar.activation(w2T[:, o:o + n], ps[0:40, 7, 256:256 + n], ACT.Copy).then_inc(s_wthi, 1)

            k_hi(0)
            w_at = P_GU
            for i in range(NG + 4):
                if 2 <= i < NG + 2:
                    o_hi(i - 2)
                if 4 <= i:
                    w_hi_t(i - 4)
                if 1 <= i <= NG:
                    pt_hi(i - 1)
                if 3 <= i < NG + 3:
                    h1_hi(i - 3)
                if i + 1 < NG:
                    k_hi(i + 1)
                if i < NG:
                    exps(i)
                if 3 <= i < NG + 3:
                    gap_exp(i - 3)
                for _ in range(2):
                    if w_at < P_DN:
                        w_hi(w_at)
                        w_at += 1
            while w_at < P_DN + 2:
                w_hi(w_at)
                w_at += 1
            for c in range(NT + 1):
                if c < NT:
                    t = tmp[:, c % 2]
                    act.wait_ge(s_g, c + 1)
                    if c >= 2:
                        act.wait_ge(s_act, c - 1)
                    nc.scalar.activation(t[:, 1], t[:, 0], ACT.Sigmoid, scale=ALPHA).then_inc(s_sig, 1)
                    act.wait_ge(s_gu, 3 * c + 3)
                    nc.scalar.activation(two(t[:, 2]), halves(2 * ((3 * c + 2) % 4)), ACT.Copy).then_inc(s_wbc, 1)
                if c >= 1:
                    act.wait_ge(s_act, c)
                    nc.scalar.activation(acts[:, c - 1, 0], tmp[:, (c - 1) % 2, 4], ACT.Copy).then_inc(s_ahi, 1)

        @block.vector
        def _(dve):
            dve.wait_ge(s_sel, 7)
            nc.vector.tensor_copy(ident_r[:, :], ident[:, :])
            nc.vector.tensor_copy(fold_r[:, :], fold_f)
            nc.vector.tensor_copy(onehot[:, :, :], onehot_f)
            nc.vector.tensor_copy(mask_l[:, :], mask_lf)
            nc.vector.tensor_copy(mask_r[:, :], mask_rf).then_inc(s_const, 1)
            nc.vector.memset(small_eps[:, :], NORM_EPS)
            nc.vector.memset(w2[:, :], 0.0)

            def x_lo(c):
                _, n, dst = pieces[c]
                dve.wait_ge(s_stage[c % STG], arrived[c])
                dve.wait_ge(s_xhi, c + 1)
                nc.vector.tensor_tensor(dst[:, 1, :], stage[:, c % STG, 0:n], f(dst[:, 0, :]),
                                        ALU.subtract).then_inc(s_xlo, 1)
            x_lo(0)
            dve.wait_ge(s_small, 16)
            nc.vector.reciprocal(inv_scale[:, :], sm[:, C_SCALE:C_SCALE + NP]).then_inc(s_smprep, 1)
            nc.vector.tensor_scalar_add(bup1[:, :], sm[:, C_BGU:C_BGU + 2 * NT].rearrange(
                "p (s u k) -> p s u k", s=NPAIR, u=2)[:, :, 1], 1.0).then_inc(s_smprep, 1)
            dve.wait_ge(s_smhi, 1)
            nc.vector.tensor_tensor(small_lo[:, :], sm[:, C_WR:C_SMALL], f(small_hi[:, :]),
                                    ALU.subtract).then_inc(s_smlo, 1)
            for c in range(1, NC):
                x_lo(c)
            dve.wait_ge(s_hthi, 1)
            nc.vector.scalar_tensor_tensor(out=two(hT[:, 2]), in0=halves(4), scalar=sm[:, C_TOKB:C_TOKB + 1],
                                           in1=two(f(hT[:, 0])), op0=ALU.add, op1=ALU.subtract).then_inc(s_htlo, 1)
            dve.wait_ge(s_hthi, 2)
            up = slice(64, 128)
            nc.vector.scalar_tensor_tensor(out=two(hT[up, 1]), in0=ps[up, 6:8, 0:TH],
                                           scalar=sm[up, C_TOKB + 1:C_TOKB + 2], in1=two(f(hT[up, 1])),
                                           op0=ALU.add, op1=ALU.subtract).then_inc(s_htlo, 1)

            def ss_lo(t):
                dve.wait_ge(s_sshi, t + 1)
                nc.vector.tensor_tensor(ss_r[:, t, 1], ss[:, t], f(ss_r[:, t, 0]), ALU.subtract).then_inc(s_sslo, 1)

            dve.wait_ge(s_smprep, 1)
            for m in range(12):
                dve.wait_ge(s_sq, m + 1)
                if m < NP:
                    nc.vector.tensor_scalar(two(qk_raw[:, m]), halves(2 * (m % 2)), inv_scale[:, m:m + 1], None,
                                            ALU.mult).then_inc(s_raw, 1)
                else:
                    nc.vector.tensor_copy(two(qk_raw[:, m]), halves(2 * (m % 2))).then_inc(s_raw, 1)
                if 1 <= m < NP:
                    if m > 1:
                        dve.wait_ge(s_ssq, m - 1)
                    nc.vector.tensor_tensor(ss[:, 0], ss[:, 0], sq[:, m % 2], ALU.add).then_inc(s_ssq, 1)
                if m == 8:
                    ss_lo(0)
            ss_lo(1)

            def v_lo(g):
                n = SIZES[g]
                dve.wait_ge(s_vhi, g + 1)
                nc.vector.tensor_tensor(V[0:n, g, 1].rearrange("p (a n) -> p a n", a=2),
                                        ps[0:n, 2 * (g % 2):2 + 2 * (g % 2), 0:PD // 2],
                                        f(V[0:n, g, 0]).rearrange("p (a n) -> p a n", a=2),
                                        ALU.subtract).then_inc(s_vlo, 1)

            def q_norm(g):
                n, o = SIZES[g], OFFS[g]
                qq = qk_raw[:, 0:NP, o:o + n]
                if g == 0:
                    dve.wait_ge(s_r, 1)
                    dve.wait_ge(s_raw, NP)
                nc.vector.tensor_tensor(qq, qq, rnorm[:, 0:1, o:o + n].to_broadcast([128, NP, n]),
                                        ALU.mult).then_inc(s_qn, 1)

            def q_split(g):
                n, o = SIZES[g], OFFS[g]
                qq = qk_raw[:, 0:NP, o:o + n]
                dve.wait_ge(s_qn, g + 1)
                if g >= 1:
                    dve.wait_ge(s_s, g)
                nc.vector.tensor_copy(Q[:, 0, :, 0:n], qq).then_inc(s_qhi, 1)
                dve.wait_ge(s_qhi, g + 1)
                nc.vector.tensor_tensor(Q[:, 1, :, 0:n], qq, f(Q[:, 0, :, 0:n]),
                                        ALU.subtract).then_inc(s_qlo, 1)

            def row_max(g):
                n = SIZES[g]
                dve.wait_ge(s_s, g + 1)
                if g >= 1:
                    dve.wait_ge(s_e, H * g)
                nc.vector.reduce_max(mx[0:n, :], ps[0:n, 0:NB, 0:HB * n].rearrange("p b (h j) -> p b h j", h=HB),
                                     X).then_inc(s_mx, 1)
                dve.wait_ge(s_mx, g + 1)
                nc.vector.tensor_scalar(negm[0:n, :], mx[0:n, :], -1.0, None, ALU.mult).then_inc(s_negm, 1)

            def sum_recip(g):
                n = SIZES[g]
                dve.wait_ge(s_e, H * (g + 1))
                if g >= 1:
                    dve.wait_ge(s_p, g)
                nc.vector.reciprocal(rinv[0:n, :], psum_e[0:n, :]).then_inc(s_rinv, 1)

            def o_lo(g):
                n = SIZES[g]
                for a in range(2):
                    dve.wait_ge(s_ohi, 2 * (g + 1))
                    r = slice(64 * a, 64 * a + 64)
                    nc.vector.tensor_tensor(oT[r, 1, :, 0:n].rearrange("p (b m) n -> p b m n", b=NB),
                                            ps[r, 3:6, 0:HB * n].rearrange("p b (m a n) -> p b m a n", m=2, a=2)[:, :, :, a],
                                            f(oT[r, 0, :, 0:n]).rearrange("p (b m) n -> p b m n", b=NB),
                                            ALU.subtract).then_inc(s_olo, 1)

            def pt_lo(g):
                n = SIZES[g]
                for b in range(NB):
                    dve.wait_ge(s_pthi, NB * g + b + 1)
                    cols = slice(b * HB * n, (b + 1) * HB * n)
                    nc.vector.tensor_tensor(PT[0:n, 1, cols], ps[0:n, 3 + b, 0:HB * n], f(PT[0:n, 0, cols]),
                                            ALU.subtract).then_inc(s_ptlo, 1)

            def h1_lo(g):
                n, o = SIZES[g], OFFS[g]
                dve.wait_ge(s_h1hi, g + 1)
                nc.vector.tensor_tensor(h1T[:, 2, o:o + n], ps[:, 7, 0:n], f(h1T[:, 0, o:o + n]),
                                        ALU.subtract).then_inc(s_h1lo, 1)
                nc.vector.tensor_tensor(h1T[up, 1, o:o + n], ps[up, 7, n:2 * n], f(h1T[up, 1, o:o + n]),
                                        ALU.subtract).then_inc(s_h1lo, 1)

            def w_lo_t(g):
                n, o = SIZES[g], OFFS[g]
                dve.wait_ge(s_wthi, g + 1)
                nc.vector.tensor_tensor(w2T[32:40, o:o + n], ps[32:40, 7, 256:256 + n], f(w2T[32:40, o:o + n]),
                                        ALU.subtract).then_inc(s_wtlo, 1)

            def layer_norm(g, src, done, src_done, st_done, mv_done, ve_done):
                n = SIZES[g]
                dve.wait_ge(src_done, g + 1)
                nc.vector.bn_stats(stats[0:n, :], src).then_inc(st_done, 1)
                dve.wait_ge(st_done, g + 1)
                nc.vector.bn_aggr(mv[0:n, :], stats[0:n, :]).then_inc(mv_done, 1)
                dve.wait_ge(mv_done, g + 1)
                nc.vector.tensor_scalar_add(var_e[0:n, :], mv[0:n, 1:2], LN_EPS).then_inc(ve_done, 1)
                dve.wait_ge(done, g + 1)

            def ln1(g):
                n = SIZES[g]
                dve.wait_ge(s_op, g + 1)
                nc.vector.tensor_tensor(y[0:n, :], ps[0:n, 6, 0:D], sm[0:n, C_BOUT:C_BOUT + D],
                                        ALU.add).then_inc(s_y, 1)
                layer_norm(g, y[0:n, :], s_rstd, s_y, s_st, s_mv, s_ve)
                nc.vector.tensor_scalar(h1[0:n, g, 0:D], y[0:n, :], mv[0:n, 0:1], rstd[0:n, 0:1],
                                        ALU.subtract, ALU.mult).then_inc(s_h1, 1)
                nc.vector.tensor_scalar(h1[0:n, g, D:D + 64], y[0:n, DA:D], mv[0:n, 0:1], rstd[0:n, 0:1],
                                        ALU.subtract, ALU.mult).then_inc(s_h1, 1)

            def router(g):
                n = SIZES[g]
                dve.wait_ge(s_rt, g + 1)
                nc.vector.tensor_tensor(lg[0:n, :], ps[0:n, 7, 384:392], sm[0:n, C_BR:C_BR + 8],
                                        ALU.add).then_inc(s_lg, 1)
                dve.wait_ge(s_lg, g + 1)
                nc.vector.max(top[0:n, :], lg[0:n, :]).then_inc(s_top, 1)
                dve.wait_ge(s_top, g + 1)
                nc.vector.tensor_tensor(rt[0:n, 2:3], top[0:n, 1:2], top[0:n, 0:1], ALU.subtract).then_inc(s_gap, 1)
                nc.vector.max_index(top_i[0:n, :], top[0:n, :], lg[0:n, :]).then_inc(s_ti, 1)
                dve.wait_ge(s_ti, 3 * g + 1)
                nc.vector.tensor_copy(rt[0:n, 0:2], top_i[0:n, 0:2]).then_inc(s_ti, 1)
                dve.wait_ge(s_egap, g + 1)
                nc.vector.tensor_scalar_add(rt[0:n, 6:7], rt[0:n, 3:4], 1.0).then_inc(s_rs, 1)
                dve.wait_ge(s_rs, g + 1)
                nc.vector.reciprocal(rt[0:n, 4:5], rt[0:n, 6:7]).then_inc(s_p1, 1)
                dve.wait_ge(s_p1, g + 1)
                nc.vector.tensor_tensor(rt[0:n, 5:6], rt[0:n, 3:4], rt[0:n, 4:5], ALU.mult).then_inc(s_p2, 1)
                dve.wait_ge(s_ti, 3 * g + 2)
                iota = sm[0:n, C_IOTA:C_IOTA + 8]
                nc.vector.tensor_scalar(sel[0:n, 0], iota, rt[0:n, 0:1], rt[0:n, 4:5], ALU.is_equal,
                                        ALU.mult).then_inc(s_ti, 1)
                dve.wait_ge(s_p2, g + 1)
                nc.vector.tensor_scalar(sel[0:n, 1], iota, rt[0:n, 1:2], rt[0:n, 5:6], ALU.is_equal,
                                        ALU.mult).then_inc(s_sel2, 1)
                dve.wait_ge(s_sel2, g + 1)
                if g >= 1:
                    dve.wait_ge(s_wt, g)
                nc.vector.tensor_tensor(w2[0:n, 0:8], sel[0:n, 0], sel[0:n, 1], ALU.add).then_inc(s_w2, 1)
                nc.vector.tensor_tensor(w2[0:n, 32:40], sel[0:n, 0], sel[0:n, 1], ALU.add).then_inc(s_w2, 1)

            q_norm(0)
            q_split(0)
            for g in range(NG):
                v_lo(g)
            for i in range(NG + 4):
                if 1 <= i <= NG:
                    sum_recip(i - 1)
                if 2 <= i < NG + 2:
                    o_lo(i - 2)
                if i + 1 < NG:
                    q_norm(i + 1)
                if i < NG:
                    row_max(i)
                if 4 <= i:
                    w_lo_t(i - 4)
                if 1 <= i <= NG:
                    pt_lo(i - 1)
                if 3 <= i < NG + 3:
                    h1_lo(i - 3)
                if i + 1 < NG:
                    q_split(i + 1)
                if 2 <= i < NG + 2:
                    ln1(i - 2)
                if 3 <= i < NG + 3:
                    router(i - 3)

            def expert_act(c):
                t = tmp[:, c % 2]
                dve.wait_ge(s_glw, c + 1)
                dve.wait_ge(s_u, c + 1)
                if c >= 1:
                    dve.wait_ge(s_ahi, c)
                nc.vector.scalar_tensor_tensor(out=t[:, 4], in0=t[:, 3], scalar=1.0 - LIMIT, in1=t[:, 1],
                                               op0=ALU.max, op1=ALU.mult).then_inc(s_act, 1)
                dve.wait_ge(s_ahi, c + 1)
                nc.vector.tensor_tensor(acts[:, c, 1], t[:, 4], f(acts[:, c, 0]), ALU.subtract).then_inc(s_alo, 1)

            dve.wait_ge(s_smprep, 2)
            for c in range(NT):
                s, k = divmod(c, 3)
                t = tmp[:, c % 2]
                cg = C_BGU + 6 * s + k
                dve.wait_ge(s_gu, 3 * c + 1)
                if c >= 2:
                    dve.wait_ge(s_alo, c - 1)
                nc.vector.tensor_scalar(two(t[:, 0]), halves(2 * (3 * c % 4)), sm[:, cg:cg + 1], LIMIT,
                                        ALU.add, ALU.min).then_inc(s_g, 1)
                dve.wait_ge(s_gu, 3 * c + 2)
                nc.vector.tensor_scalar(two(t[:, 3]), halves(2 * ((3 * c + 1) % 4)), bup1[:, c:c + 1], LIMIT + 1,
                                        ALU.add, ALU.min).then_inc(s_u, 1)
                if c >= 1:
                    expert_act(c - 1)
            expert_act(NT - 1)

            for g in range(NG):
                n = SIZES[g]
                zz = z[0:n, g % 2, :]
                dve.wait_ge(s_dn, g + 1)
                nc.vector.tensor_tensor(zz, ps[0:n, g, 0:D], h1[0:n, g, 0:D], ALU.add).then_inc(s_z, 1)
                layer_norm(g, zz, s_zrstd, s_z, s_zst, s_zmv, s_zve)
                if g >= 2:
                    dve.wait_ge(s_out[g % 2], 16 * (g // 2))
                nc.vector.tensor_scalar(res[0:n, g % 2, :], zz, mv[0:n, 0:1], rstd[0:n, 0:1],
                                        ALU.subtract, ALU.mult).then_inc(s_res, 1)

        @block.tensor
        def _(pe):
            mm = nc.tensor.matmul

            for c in range(NC):
                pe.wait_ge(s_xlo, c + 1)
                hi, lo = xw[:, c % XR, 0], xw[:, c % XR, 1]
                for wx, px in ((hi, hi), (hi, lo), (lo, hi)):
                    for t in range(2):
                        for a in range(2):
                            last = mm(ps[:, 4 + 2 * t + a, 0:TH], wx[:, T + 128 * t:T + 128 * t + 128],
                                      px[:, TH * a:TH * a + TH], start=(c == 0 and wx is hi and px is hi),
                                      stop=(c == NC - 1 and wx is lo))
                last.then_inc(s_tok, 1)

            def wide(bank, w_a, w_b, x, a):
                cols = slice(TH * a, TH * a + TH)
                out_ap = ps[:, bank, 0:TH]
                mm(out_ap, w_a(0), x[:, 0, cols], start=True, stop=False)
                mm(out_ap, w_a(1), x[:, 0, cols], start=False, stop=False)
                mm(out_ap, w_a(0), x[:, 2, cols], start=False, stop=False)
                mm(out_ap, w_b(0), x[:, 1, cols], start=False, stop=False)
                return mm(out_ap, w_b(1), x[:, 1, cols], start=False, stop=True)

            def norm_sum(t):
                pe.wait_ge(s_sslo, t + 1)
                for a in range(2):
                    for k in range(2):
                        last = mm(ps[:, 4 + 2 * t + a, 0:TH], fold_r[:, :], ss_r[:, t, k, TH * a:TH * a + TH],
                                  start=(k == 0), stop=(k == 1))
                last.then_inc(s_nsum, 1)

            pe.wait_ge(s_htlo, 2)
            pe.wait_ge(s_const, 1)
            for m in range(12):
                s, p = divmod(m, NP)
                pe.wait_ge(s_wlo, w_ready(P_QKV + 2 * s + 1))
                if m >= 2:
                    pe.wait_ge(s_raw, m - 1)
                cols = slice(128 * p, 128 * p + 128)
                for a in range(2):
                    last = wide(2 * (m % 2) + a, lambda k: wqkv[:, s, 0, k, cols],
                                lambda k: wqkv[:, s, 1, k, cols], hT, a)
                last.then_inc(s_qk, 1)
                if m == 10:
                    norm_sum(0)

            def v_proj(g):
                n, o = SIZES[g], OFFS[g]
                if g == 0:
                    pe.wait_ge(s_wlo, w_ready(P_QKV + 5))
                if g < 2:
                    pe.wait_ge(s_raw, 11 + g)
                else:
                    pe.wait_ge(s_vlo, g - 1)
                tok = slice(o, o + n)
                for a in range(2):
                    cols = slice(PD // 2 * a, PD // 2 * (a + 1))
                    out_ap = ps[0:n, 2 * (g % 2) + a, 0:PD // 2]
                    mm(out_ap, hT[:, 0, tok], wqkv[:, 2, 0, 0, cols], start=True, stop=False)
                    mm(out_ap, hT[:, 0, tok], wqkv[:, 2, 0, 1, cols], start=False, stop=False)
                    mm(out_ap, hT[:, 2, tok], wqkv[:, 2, 0, 0, cols], start=False, stop=False)
                    mm(out_ap, hT[:, 1, tok], wqkv[:, 2, 1, 0, cols], start=False, stop=False)
                    last = mm(out_ap, hT[:, 1, tok], wqkv[:, 2, 1, 1, cols], start=False, stop=True)
                last.then_inc(s_v, 1)

            v_proj(0)
            norm_sum(1)
            for g in range(1, NG):
                v_proj(g)

            def scores(g):
                n = SIZES[g]
                pe.wait_ge(s_qlo, g + 1)
                pe.wait_ge(s_klo, 2 * (g + 1))
                if g == 0:
                    pe.wait_ge(s_vlo, NG)
                for b in range(NB):
                    if g >= 1:
                        pe.wait_ge(s_e, H * (g - 1) + HB * (b + 1))
                    mm(ps[0:n, b, 0:HB * n], mask_l[:, 0:n],
                       mask_r[:, :].rearrange("p (h j) -> p h j", h=HB)[:, :, 0:n], start=True, stop=False,
                       skip_group_check=True)
                    for j in range(2):
                        m = 2 * b + j
                        for qp, kp in ((0, 0), (0, 1), (1, 0)):
                            last = mm(ps[0:n, b, 2 * n * j:2 * n * (j + 1)], Q[:, qp, m, 0:n], K[:, kp, m, :, 0:n],
                                      start=False, stop=(qp == 1), skip_group_check=True)
                last.then_inc(s_s, 1)

            def p_transpose(g):
                n = SIZES[g]
                pe.wait_ge(s_p, g + 1)
                if g >= 1:
                    pe.wait_ge(s_olo, 2 * g)
                for h in range(H):
                    last = nc.tensor.transpose(ps[0:n, 3 + h // HB, (h % HB) * n:(h % HB + 1) * n],
                                               Pr[0:n, h * n:(h + 1) * n], ident[0:n, 0:n])
                last.then_inc(s_pt, 1)

            def weighted(g):
                n = SIZES[g]
                for p in range(NP):
                    b = p // 2
                    pe.wait_ge(s_ptlo, NB * g + b + 1)
                    pe.wait_ge(s_vlo, g + 1)
                    out_ap = ps[:, 3 + b, (p % 2) * 2 * n:(p % 2 + 1) * 2 * n]
                    for vp, pp in ((0, 0), (0, 1), (1, 0)):
                        last = mm(out_ap, V[0:n, g, vp, 128 * p:128 * p + 128], PT[0:n, pp, 2 * p * n:2 * (p + 1) * n],
                                  start=(vp == 0 and pp == 0), stop=(vp == 1))
                last.then_inc(s_pv, 1)

            def project(g):
                n, o = SIZES[g], OFFS[g]
                pe.wait_ge(s_olo, 2 * (g + 1))
                pe.wait_ge(s_wlo, w_ready(P_OUT))
                if g >= 1:
                    pe.wait_ge(s_y, g)
                tok = slice(o, o + n)
                for p in range(NP):
                    for op_, wp in ((0, 0), (0, 1), (1, 0)):
                        mm(ps[0:n, 6, 0:D], oT[:, op_, p, 0:n], wout[:, wp, p, :],
                           start=(p == 0 and op_ == 0 and wp == 0), stop=False)
                mm(ps[0:n, 6, 0:DA], hT[:, 0, tok], ident_r[:, :], start=False, stop=False)
                mm(ps[0:n, 6, 0:DA], hT[:, 2, tok], ident_r[:, :], start=False, stop=False)
                mm(ps[0:n, 6, DA:D], hT[:, 1, tok], fold_r[:, 0:DB], start=False, stop=True).then_inc(s_op, 1)

            def h1_transpose(g):
                n = SIZES[g]
                pe.wait_ge(s_h1, 2 * (g + 1))
                if g >= 1:
                    pe.wait_ge(s_wtlo, g)
                for k in range(2):
                    last = nc.tensor.transpose(ps[:, 7, k * n:(k + 1) * n], h1[0:n, g, 128 * k:128 * k + 128],
                                               ident[0:n, 0:n])
                last.then_inc(s_ht1, 1)

            def logits(g):
                n, o = SIZES[g], OFFS[g]
                tok = slice(o, o + n)
                pe.wait_ge(s_h1lo, 2 * (g + 1))
                out_ap = ps[0:n, 7, 384:392]
                a_hi, a_lo, b_hi, b_lo = small_hi[:, 0:8], small_lo[:, 0:8], small_hi[:, 8:16], small_lo[:, 8:16]
                mm(out_ap, h1T[:, 0, tok], a_hi, start=True, stop=False)
                mm(out_ap, h1T[:, 0, tok], a_lo, start=False, stop=False)
                mm(out_ap, h1T[:, 2, tok], a_hi, start=False, stop=False)
                mm(out_ap, h1T[:, 1, tok], b_hi, start=False, stop=False)
                mm(out_ap, h1T[:, 1, tok], b_lo, start=False, stop=True).then_inc(s_rt, 1)

            def w_transpose(g):
                n = SIZES[g]
                pe.wait_ge(s_w2, 2 * (g + 1))
                nc.tensor.transpose(ps[0:40, 7, 256:256 + n], w2[0:n, :], ident[0:n, 0:n]).then_inc(s_wt, 1)

            pe.wait_ge(s_smlo, 1)
            for i in range(NG + 4):
                if i < NG:
                    scores(i)
                if 4 <= i:
                    w_transpose(i - 4)
                if 1 <= i <= NG:
                    p_transpose(i - 1)
                if 3 <= i < NG + 3:
                    h1_transpose(i - 3)
                if 2 <= i < NG + 2:
                    project(i - 2)
                if 3 <= i < NG + 3:
                    logits(i - 3)
                if 1 <= i <= NG:
                    weighted(i - 1)

            pe.wait_ge(s_wtlo, NG)
            for c in range(NT):
                s, k = divmod(c, 3)
                pe.wait_ge(s_wlo, w_ready(P_GU + 2 * s + 1))
                for u in range(3):
                    use = 3 * c + u
                    bank = 2 * (use % 4)
                    if use >= 4:
                        cc, uu = divmod(use - 4, 3)
                        pe.wait_ge((s_g, s_u, s_wbc)[uu], cc + 1)
                    for a in range(2):
                        if u < 2:
                            cols = slice(384 * u + 128 * k, 384 * u + 128 * k + 128)
                            last = wide(bank + a, lambda j: wgu[:, s, 0, j, cols], lambda j: wgu[:, s, 1, j, cols],
                                        h1T, a)
                        else:
                            first = 256 * s + (0, 128, 64)[k]
                            w = onehot[:, :, :].rearrange("p e n -> p (e n)")[:, first:first + 128]
                            last = mm(ps[:, bank + a, 0:TH], w, w2T[:, TH * a:TH * a + TH], start=True, stop=True)
                    last.then_inc(s_gu, 1)

            pe.wait_ge(s_wlo, w_ready(P_DN + 1))
            pe.wait_ge(s_wbc, NT)
            pe.wait_ge(s_u, NT)
            for g in range(NG):
                n, o = SIZES[g], OFFS[g]
                tok = slice(o, o + n)
                out_ap = ps[0:n, g, 0:D]
                mm(out_ap, w2T[:, tok], small_hi[0:40, 16:16 + D], start=True, stop=False)
                mm(out_ap, w2T[:, tok], small_lo[0:40, 16:16 + D], start=False, stop=False)
                for c in range(NT):
                    pe.wait_ge(s_alo, c + 1)
                    w = wd[:, c // 6, :, D * (c % 6):D * (c % 6) + D]
                    for ap_, wp in ((0, 0), (0, 1), (1, 0)):
                        last = mm(out_ap, acts[:, c, ap_, tok], w[:, wp], start=False,
                                  stop=(c == NT - 1 and ap_ == 1))
                last.then_inc(s_dn, 1)


def kernel(x, L0_tok_W, L0_tok_b, L0_attn_w_qkv, L0_attn_w_out, L0_attn_b_out, L0_attn_scale, L0_ffn_Wr, L0_ffn_br,
           L0_ffn_Wgu, L0_ffn_bgu, L0_ffn_Wd, L0_ffn_bd):
    import numpy as np
    import concourse.bacc as bacc
    from concourse.bass_utils import run_bass_kernel_spmd

    def arr(a):
        return np.asarray(a)

    p = 16
    xT = arr(x).reshape(B, 6, p, 6, p, 3).transpose(2, 4, 5, 0, 1, 3).reshape(NC, 128, T)
    w_tok = arr(L0_tok_W).reshape(NC, 128, D)
    w_tok = np.concatenate([w_tok, w_tok[:, :, DA:]], axis=2)
    wqkvT = arr(L0_attn_w_qkv).T.reshape(D, 3, PD).transpose(1, 0, 2)
    w_outT = arr(L0_attn_w_out).T.reshape(NC, 128, D).transpose(1, 0, 2).reshape(128, NC * D)

    def tiles(a):
        lead = a.shape[0]
        a = a.reshape(lead, NPAIR, 2, 2, FI)
        full = a[..., :DA].transpose(0, 1, 3, 2, 4).reshape(lead, NPAIR, 2, 2 * DA)
        rest = a[..., DA:].transpose(0, 1, 3, 2, 4).reshape(lead, NPAIR, 2, 2 * DB)
        return np.concatenate([full, rest], axis=3).reshape(lead, NPAIR, 6 * 128)
    w_gu = tiles(arr(L0_ffn_Wgu).transpose(1, 0, 2).reshape(D, E * 2 * FI)).transpose(1, 0, 2)
    b_gu = tiles(arr(L0_ffn_bgu).reshape(1, E * 2 * FI)).reshape(NPAIR * 6, 128).T
    wd = arr(L0_ffn_Wd).reshape(NPAIR, 2, FI, D)
    wd = np.concatenate([wd[:, :, :DA].reshape(NPAIR, 2 * DA, D), wd[:, :, DA:].reshape(NPAIR, 2 * DB, D)], axis=1)
    wd = wd.reshape(2, 6, 128, D).transpose(0, 2, 1, 3).reshape(2, 128, 6 * D)

    small = np.zeros((128, C_SMALL), np.float32)
    tok_b = arr(L0_tok_b)
    small[:, C_TOKB] = tok_b[:DA]
    small[:DB, C_TOKB + 1] = small[DB:, C_TOKB + 1] = tok_b[DA:]
    small[:, C_SCALE:C_SCALE + NP] = np.repeat(arr(L0_attn_scale).reshape(NP, 2).T, DH, axis=0)
    small[:, C_BR:C_BR + E] = arr(L0_ffn_br)
    small[:, C_BGU:C_BGU + 2 * NT] = b_gu
    small[:, C_IOTA:C_IOTA + E] = np.arange(E)
    small[:, C_BOUT:C_BOUT + D] = arr(L0_attn_b_out)
    small[:, C_WR:C_WR + E] = arr(L0_ffn_Wr)[:DA]
    small[:DB, C_WR + E:C_WR + 2 * E] = small[DB:, C_WR + E:C_WR + 2 * E] = arr(L0_ffn_Wr)[DA:]
    small[0:E, C_BD:C_BD + D] = small[32:32 + E, C_BD:C_BD + D] = arr(L0_ffn_bd)

    ins = {"xT": xT, "w_tok": w_tok, "w_qkv_a": wqkvT[:, :DA], "w_qkv_b": wqkvT[:, DA:], "w_out": w_outT,
           "w_gu_a": w_gu[:, :DA], "w_gu_b": w_gu[:, DA:], "w_down": wd, "small": small}
    nc = bacc.Bacc("TRN2", target_bir_lowering=False, num_devices=1)
    arrays, aps = {}, []
    for name, a in ins.items():
        arrays[name] = np.ascontiguousarray(a)
        aps.append(nc.dram_tensor(name, a.shape, mybir.dt.float32, kind="ExternalInput").ap())
    out = nc.dram_tensor("out", (T, D), mybir.dt.float32, kind="ExternalOutput").ap()
    vit_layer(nc, *aps, out)
    r = run_bass_kernel_spmd(nc, [arrays], core_ids=[0])
    return r.results[0]["out"].reshape(B, SEQ, D)
```

```python
import math

import concourse.bass as bass
from concourse import mybir
from contextlib import ExitStack


D = 192
DA, DB = 128, 64
PD, NC = 768, 6
B, SEQ = 16, 36
T = B * SEQ
TH = T // 2
H, DH = 12, 64
NP = H // 2
E, FI = 8, 192
NPAIR = E // 2
NT = 3 * NPAIR
IMG = 3
GRP = IMG * SEQ
SIZES = [GRP] * (B // IMG) + [SEQ * (B % IMG)] * (B % IMG > 0)
GU_ORDER = [3, 0, 1, 2]
OFFS = [GRP * g for g in range(len(SIZES))]
NG = len(SIZES)
BANK = 512
HB = 4
NB = H // HB
LN_EPS, NORM_EPS = 1e-5, 1e-8
ALPHA, LIMIT = 1.702, 7.0
MASKED = -2.0 ** 126

C_TOKB, C_SCALE, C_BR, C_BGU, C_IOTA, C_WR, C_BD = 0, 2, 8, 16, 40, 48, 64
C_SMALL = C_BD + D
BOUT_ROW = 64

STG = 4
STGW = 768
XW = T + 2 * 128
TD = 96
ND = T // TD


def vit_layer(nc, xT, w_tok, w_qkv_a, w_qkv_b, w_out, w_gu_a, w_gu_b, w_down, small, out):
    f32, f32r, bf16, u32 = mybir.dt.float32, mybir.dt.float32r, mybir.dt.bfloat16, mybir.dt.uint32
    ALU = mybir.AluOpType
    ACT = mybir.ActivationFunctionType
    X = mybir.AxisListType.X

    ctx = ExitStack()
    with ctx:
        def sb(name, shape, dt=f32):
            return ctx.enter_context(nc.sbuf_tensor(name, shape, dt))

        def sem(name):
            return ctx.enter_context(nc.semaphore(name))

        def f(ap):
            return ap.bitcast(f32)

        reg_a = sb("reg_a", [128, 15696], f32r)
        reg_b = sb("reg_b", [128, 12288], f32r)
        reg_c = sb("reg_c", [128, 5328], f32r)
        h1T = sb("h1T", [128, 3, T], f32r)
        w2T = sb("w2T", [40, T], f32r)
        onehot = sb("onehot", [40, E, 128], f32r)
        ident_r = sb("ident_r", [128, 128], f32r)
        fold_r = sb("fold_r", [128, 128], f32r)
        small_hi = sb("small_hi", [128, 16 + D], f32r)
        small_lo = sb("small_lo", [128, 16 + D], f32r)
        mask_l = sb("mask_l", [128, GRP], bf16)
        mask_r = sb("mask_r", [128, HB * GRP], bf16)

        xw = reg_a[:, 0:NC * 2 * XW].rearrange("p (s k n) -> p s k n", s=NC, k=2)
        V = reg_a[:, 0:NG * 2 * PD].rearrange("p (g k n) -> p g k n", g=NG, k=2)
        Q = reg_a[:, 9216:9216 + 2 * NP * GRP].rearrange("p (k m n) -> p k m n", k=2, m=NP)
        K = reg_a[:, 10512:10512 + 4 * NP * GRP].rearrange("p (k m a n) -> p k m a n", k=2, m=NP, a=2)
        PT = reg_a[:, 13104:13104 + 2 * H * GRP].rearrange("p (k n) -> p k n", k=2)
        acts = reg_a[:, 0:2 * NT * T].rearrange("p (a c k n) -> p a c k n", a=2, c=NT, k=2)
        wqkv = reg_b[:, 0:4 * 3 * PD].rearrange("p (s c k n) -> p s c k n", s=3, c=2, k=2)
        wgu = reg_b[:, :].rearrange("p (s c k n) -> p s c k n", s=NPAIR, c=2, k=2)
        wout = reg_c[:, 0:2 * NC * D].rearrange("p (s k c n) -> p s k c n", s=2, k=2, c=3)
        hT = reg_c[:, 2304:2304 + 3 * T].rearrange("p (k n) -> p k n", k=3)
        oT = reg_c[:, 4032:4032 + 2 * NP * GRP].rearrange("p (k m n) -> p k m n", k=2, m=NP)
        wd = reg_c[:, 0:2 * NT * D].rearrange("p (s k c n) -> p s k c n", s=4, k=2, c=3)

        stage = sb("stage", [128, STG, STGW])
        reg_q = sb("reg_q", [128, 12 * T])
        qk_raw = reg_q[:, :].rearrange("p (m n) -> p m n", m=12)
        xstage = reg_q[:, 0:NC * XW].rearrange("p (c n) -> p c n", c=NC)
        tmp = reg_q[:, :].rearrange("p (s k n) -> p s k n", s=4, k=6)
        rnorm = sb("rnorm", [128, 2, T])
        Pr = sb("Pr", [128, 2, H * GRP])
        h1 = sb("h1", [128, 2, 256])
        sq = Pr[:, 0, 0:2 * T].rearrange("p (k n) -> p k n", k=2)
        ss = Pr[:, 1, 0:2 * T].rearrange("p (k n) -> p k n", k=2)
        ss_r = reg_a[:, 13104:13104 + 4 * T].rearrange("p (t k n) -> p t k n", t=2, k=2)
        sm = sb("sm", [128, C_SMALL])
        inv_scale = sb("inv_scale", [128, NP])
        bup1 = sb("bup1", [128, NT])
        small_eps = sb("small_eps", [128, 1])
        ident = sb("ident", [128, 128])
        half = sb("half", [128, 1])
        euler = sb("euler", [128, 1])
        negm = sb("negm", [128, H])
        mx = sb("mx", [128, H])
        psum_e = sb("psum_e", [128, H])
        rinv = sb("rinv", [128, H])
        stats = sb("stats", [128, 6])
        mv = sb("mv", [128, 2])
        var_e = sb("var_e", [128, 1])
        rstd = sb("rstd", [128, 1])
        lg = sb("lg", [128, 8])
        top = sb("top", [128, 8])
        top_i = sb("top_i", [128, 8], u32)
        rt = sb("rt", [128, 8])
        sel = sb("sel", [128, 2, 8])
        w2 = sb("w2", [128, 40])
        res = rnorm[:, 1, 0:2 * D].rearrange("p (k n) -> p k n", k=2)
        onehot_f = Pr[0:40, 0, 0:E * 128].rearrange("p (e n) -> p e n", e=E)
        fold_f = rnorm[:, 0, 0:128]
        mask_lf = rnorm[:, 0, 128:128 + GRP]
        mask_rf = rnorm[:, 1, 0:HB * GRP]

        ps = ctx.enter_context(nc.psum_tensor("ps", [128, 8, BANK], f32))

        def halves(bank):
            return ps[:, bank:bank + 2, 0:TH]

        def two(ap):
            return ap.rearrange("p (a n) -> p a n", a=2)

        s_stage = [sem(f"s_stage{i}") for i in range(STG)]
        s_xst = [sem(f"s_xst{i}") for i in range(NC)]
        s_small = sem("s_small")
        s_out = [sem(f"s_out{i}") for i in range(2)]
        (s_fill, s_sel, s_const, s_smprep, s_smhi, s_smlo, s_xhi, s_xlo, s_whi, s_wlo, s_w6lo, s_tok, s_hthi, s_htlo,
         s_qk, s_raw, s_sq, s_ssq, s_ssk, s_sshi, s_sslo, s_nsum, s_nsqrt, s_nln, s_r, s_v, s_vhi, s_vlo,
         s_qn, s_kn, s_qhi, s_qlo, s_khi, s_klo, s_s, s_mx, s_negm, s_e, s_rinv, s_p, s_pt, s_pthi, s_ptlo, s_pv,
         s_ohi, s_olo, s_op, s_st, s_mv, s_ve, s_rstd, s_h1, s_ht1, s_h1hi, s_h1lo, s_rt, s_lg, s_top, s_ti,
         s_gap, s_egap, s_rs, s_p1, s_p2, s_sel2, s_w2, s_wt, s_wthi, s_wtlo, s_gu, s_g, s_sig, s_glu, s_wbc,
         s_glw, s_u, s_act, s_ahi, s_alo, s_dn, s_zst, s_zmv, s_zve, s_zrstd, s_res) = [
            sem(n) for n in (
                "s_fill s_sel s_const s_smprep s_smhi s_smlo s_xhi s_xlo s_whi s_wlo s_w6lo s_tok s_hthi s_htlo "
                "s_qk s_raw s_sq s_ssq s_ssk s_sshi s_sslo s_nsum s_nsqrt s_nln s_r s_v s_vhi s_vlo "
                "s_qn s_kn s_qhi s_qlo s_khi s_klo s_s s_mx s_negm s_e s_rinv s_p s_pt s_pthi s_ptlo s_pv "
                "s_ohi s_olo s_op s_st s_mv s_ve s_rstd s_h1 s_ht1 s_h1hi s_h1lo s_rt s_lg s_top s_ti "
                "s_gap s_egap s_rs s_p1 s_p2 s_sel2 s_w2 s_wt s_wthi s_wtlo s_gu s_g s_sig s_glu s_wbc "
                "s_glw s_u s_act s_ahi s_alo s_dn s_zst s_zmv s_zve s_zrstd s_res").split()]

        pieces = []
        for c in range(NC):
            pieces.append(([(xT[c], 0, 128, 0, T), (w_tok[c], 0, 128, T, 256)], XW, xstage[:, c], xw[:, c]))

        def add_weight(loads, n, dst):
            pieces.append((loads, n, stage[:, (len(pieces) - NC) % STG, 0:n], dst))
        for s in range(3):
            add_weight([(w_qkv_a[s], 0, 128, 0, PD)], PD, wqkv[:, s, 0])
            add_weight([(w_qkv_b[s], 0, 64, 0, PD), (w_qkv_b[s], 64, 128, 0, PD)], PD, wqkv[:, s, 1])
        for s in range(2):
            add_weight([(w_out[s], 0, 128, 0, 3 * D)], 3 * D, wout[:, s].rearrange("p k c n -> p k (c n)"))
        for s in GU_ORDER:
            add_weight([(w_gu_a[s], 0, 128, 0, 768)], 768, wgu[:, s, 0])
            add_weight([(w_gu_b[s], 0, 64, 0, 768), (w_gu_b[s], 64, 128, 0, 768)], 768, wgu[:, s, 1])
        for s in range(4):
            add_weight([(w_down[s], 0, 128, 0, 3 * D)], 3 * D, wd[:, s].rearrange("p k c n -> p k (c n)"))
        P_QKV, P_OUT = NC, NC + 6
        P_GU = P_OUT + 2
        P_DN = P_GU + 2 * NPAIR
        arrived = []
        for k, (loads, _, _, _) in enumerate(pieces):
            arrived.append(16 * len(loads) + (arrived[k - STG] if k >= NC + STG else 0))

        def arrival(k):
            return (s_xst[k] if k < NC else s_stage[(k - NC) % STG]), arrived[k]

        def w_ready(k):
            return k - NC

        uses = [("qk", m) for m in range(11)] + [("sum", 0), ("qk", 11), ("v", 0), ("sum", 1)]
        uses += [("v", g) for g in range(1, NG)]
        slot = {use: 2 * (n % 4) for n, use in enumerate(uses)}

        def slot_read(use):
            n = uses.index(use)
            if n < 4:
                return None
            kind, j = uses[n - 4]
            return {"qk": s_raw, "sum": s_nsqrt, "v": s_vlo}[kind], j + 1

        def down_bank(j):
            return 3 + j if j < ND // 2 else j - ND // 2

        def gu_bank(a, c, u):
            return 6 + u if a == 1 and c % 2 and u < 2 else u

        block = ctx.enter_context(nc.Block())

        @block.sync
        def _(sp):
            for k, (loads, _, place, _) in enumerate(pieces):
                if k == NC + STG:
                    sp.wait_ge(s_w6lo, 1)
                elif k > NC + STG:
                    sp.wait_ge(s_wlo, w_ready(k - STG))
                for src, p0, p1, c0, n in loads:
                    sp.dma_start(place[p0:p1, c0:c0 + n], src).then_inc(arrival(k)[0], 16)
                if k == 0:
                    sp.dma_start(sm[:, :], small).then_inc(s_small, 16)
            for j in range(ND):
                sp.wait_ge(s_res, j + 1)
                sp.dma_start(out[TD * j:TD * j + TD, :], res[0:TD, j % 2, :]).then_inc(s_out[j % 2], 16)
            for i in range(2):
                sp.wait_ge(s_out[i], 16 * (ND // 2))

        @block.gpsimd
        def _(pool):
            for t, value in ((ident[:, :], 0.0), (fold_f, 0.0), (onehot_f, 0.0), (mask_lf, 0.0), (half[:, :], -0.5),
                             (euler[:, :], math.e)):
                nc.gpsimd.memset(t, value).then_inc(s_fill, 1)
            nc.gpsimd.memset(mask_rf, MASKED).then_inc(s_fill, 1)
            pool.wait_ge(s_fill, 7)
            nc.gpsimd.memset(f(K[64:128, :, :, 0]), 0.0).then_inc(s_fill, 1)
            pool.wait_ge(s_fill, 8)
            nc.gpsimd.memset(f(K[0:64, :, :, 1]), 0.0).then_inc(s_fill, 1)
            pool.wait_ge(s_fill, 9)

            def fill(ap, base, pattern, value, n):
                pool.wait_ge(s_sel, n)
                nc.gpsimd.affine_select(out=ap, in_=ap, compare_op=ALU.not_equal, fill=value, base=base,
                                        pattern=pattern, channel_multiplier=1).then_inc(s_sel, 1)
            nc.gpsimd.affine_select(out=ident[:, :], in_=ident[:, :], compare_op=ALU.not_equal, fill=1.0, base=0,
                                    pattern=[[-1, 128]], channel_multiplier=1).then_inc(s_sel, 1)
            fold3 = fold_f.rearrange("p (a n) -> p a n", a=2)
            fill(fold3, 0, [[0, 2], [-1, 64]], 1.0, 1)
            fill(fold3, -64, [[0, 2], [-1, 64]], 1.0, 2)
            fill(mask_lf.rearrange("p (a n) -> p a n", a=IMG), 0, [[-1, IMG], [0, SEQ]], 1.0, 3)
            fill(mask_rf.rearrange("p (h a n) -> p h a n", h=HB, a=IMG), 0, [[0, HB], [-1, IMG], [0, SEQ]], 0.0, 4)
            fill(onehot_f, 0, [[-1, E], [0, 128]], 1.0, 5)
            fill(onehot_f, -32, [[-1, E], [0, 128]], 1.0, 6)

            def w_lo(k):
                _, n, place, dst = pieces[k]
                pool.wait_ge(*arrival(k))
                pool.wait_ge(s_whi, w_ready(k) + 1)
                if P_GU + 2 <= k:
                    pool.wait_ge(s_v, NG)
                if P_DN <= k:
                    pool.wait_ge(s_op, NG)
                nc.gpsimd.tensor_tensor(dst[:, 1, :], place, f(dst[:, 0, :]), ALU.subtract).then_inc(s_wlo, 1)
            for k in range(P_QKV + 1, P_QKV + 6):
                w_lo(k)
            for m in range(7, 12):
                pool.wait_ge(s_sq, m + 1)
                if m > 7:
                    pool.wait_ge(s_ssk, m - 7)
                nc.gpsimd.tensor_tensor(ss[:, 1], ss[:, 1], sq[:, m % 2], ALU.add).then_inc(s_ssk, 1)
            for k in range(P_OUT, P_GU + 2):
                w_lo(k)

            def k_norm(g):
                n, o = SIZES[g], OFFS[g]
                kk = qk_raw[:, NP:2 * NP, o:o + n]
                if g == 0:
                    pool.wait_ge(s_r, 2)
                    pool.wait_ge(s_raw, 12)
                nc.gpsimd.tensor_tensor(kk, kk, rnorm[:, 1:2, o:o + n].to_broadcast([128, NP, n]),
                                        ALU.mult).then_inc(s_kn, 1)

            def k_lo(g):
                n, o = SIZES[g], OFFS[g]
                pool.wait_ge(s_kn, g + 1)
                pool.wait_ge(s_khi, 2 * (g + 1))
                if g >= 1:
                    pool.wait_ge(s_s, g)
                for a in range(2):
                    r = slice(64 * a, 64 * a + 64)
                    if a == 1:
                        pool.wait_ge(s_klo, 2 * g + 1)
                    nc.gpsimd.tensor_tensor(K[r, 1, :, a, 0:n], qk_raw[r, NP:2 * NP, o:o + n], f(K[r, 0, :, a, 0:n]),
                                            ALU.subtract).then_inc(s_klo, 1)
                pool.wait_ge(s_klo, 2 * g + 2)

            def probs(g):
                n = SIZES[g]
                pool.wait_ge(s_rinv, g + 1)
                pool.wait_ge(s_e, H * (g + 1))
                pp = Pr[0:n, g % 2, 0:H * n].rearrange("p (h j) -> p h j", h=H)
                nc.gpsimd.tensor_tensor(pp, pp, rinv[0:n, :].unsqueeze(2).to_broadcast([n, H, n]),
                                        ALU.mult).then_inc(s_p, 1)

            def root(g, n, ve, done):
                pool.wait_ge(ve, g + 1)
                nc.gpsimd.tensor_tensor(rstd[0:n, :], var_e[0:n, :], half[0:n, :], ALU.pow).then_inc(done, 1)

            def gap_exp(g):
                n = SIZES[g]
                pool.wait_ge(s_gap, g + 1)
                nc.gpsimd.tensor_tensor(rt[0:n, 3:4], euler[0:n, :], rt[0:n, 2:3], ALU.pow).then_inc(s_egap, 1)

            def expert(a, c):
                u = NT * a + c
                t = tmp[:, u % 4]
                pool.wait_ge(s_g, u + 1)
                pool.wait_ge(s_sig, u + 1)
                nc.gpsimd.tensor_tensor(t[:, 1], t[:, 0], t[:, 1], ALU.mult).then_inc(s_glu, 1)
                pool.wait_ge(s_wbc, u + 1)
                pool.wait_ge(s_glu, u + 1)
                nc.gpsimd.tensor_tensor(t[:, 1], t[:, 1], t[:, 2], ALU.mult).then_inc(s_glw, 1)

            k_norm(0)
            k_lo(0)
            for i in range(NG + 4):
                if 1 <= i <= NG:
                    probs(i - 1)
                if i + 1 < NG:
                    k_norm(i + 1)
                    k_lo(i + 1)
                if 2 <= i < NG + 2:
                    root(i - 2, SIZES[i - 2], s_ve, s_rstd)
                if 3 <= i < NG + 3:
                    gap_exp(i - 3)
                if i < 2 * NPAIR - 2:
                    w_lo(P_GU + 2 + i)
                if i >= NG:
                    for c in range(3 * (i - NG), 3 * (i - NG) + 3):
                        expert(0, c)
            w_lo(P_DN)
            for c in range(NT):
                expert(1, c)
                if c % 3 == 1 and c < 9:
                    w_lo(P_DN + 1 + c // 3)
            for j in range(ND):
                root(j, TD, s_zve, s_zrstd)

        @block.scalar
        def _(act):
            def w_hi(k):
                _, n, place, dst = pieces[k]
                act.wait_ge(*arrival(k))
                if k >= P_DN:
                    act.wait_ge(s_op, NG)
                elif k >= P_GU + 2:
                    act.wait_ge(s_v, NG)
                nc.scalar.activation(dst[:, 0, :], place, ACT.Copy).then_inc(s_xhi if k < NC else s_whi, 1)
            w_hi(0)
            act.wait_ge(s_small, 16)
            nc.scalar.activation(small_hi[:, :], sm[:, C_WR:C_SMALL], ACT.Copy).then_inc(s_smhi, 1)
            for c in range(1, NC):
                w_hi(c)
            w_hi(P_QKV)
            w_hi(P_QKV + 1)
            act.wait_ge(s_tok, NC)
            for t in range(2):
                nc.scalar.activation(two(hT[:, t]), halves(4 + 2 * t), ACT.Identity,
                                     bias=sm[:, C_TOKB + t:C_TOKB + t + 1]).then_inc(s_hthi, 1)

            def root(t):
                act.wait_ge(s_nsum, t + 1)
                nc.scalar.activation(two(rnorm[:, t]), halves(slot["sum", t]), ACT.Sqrt).then_inc(s_nsqrt, 1)

            def ss_hi(t):
                act.wait_ge(s_ssk if t else s_ssq, 5)
                nc.scalar.activation(ss_r[:, t, 0], ss[:, t], ACT.Copy).then_inc(s_sshi, 1)

            act.wait_ge(s_const, 1)
            w_next = P_QKV + 2
            for m in range(12):
                if m == 7:
                    ss_hi(0)
                act.wait_ge(s_qk, m + 1)
                if m % 6 >= 3:
                    act.wait_ge(s_ssk if m >= 6 else s_ssq, m % 6 - 2)
                dst = ss[:, m // 6] if m % 6 == 0 else sq[:, m % 2]
                if m in (7, 8):
                    act.wait_ge(s_ssq, 5)
                nc.scalar.activation(two(dst), halves(slot["qk", m]), ACT.Square).then_inc(s_sq, 1)
                if w_next < P_GU + 2 and m != 6:
                    w_hi(w_next)
                    w_next += 1
            root(0)

            def v_hi(g):
                n = SIZES[g]
                act.wait_ge(s_v, g + 1)
                nc.scalar.activation(V[0:n, g, 0].rearrange("p (a n) -> p a n", a=2),
                                     ps[0:n, slot["v", g]:slot["v", g] + 2, 0:PD // 2], ACT.Copy).then_inc(s_vhi, 1)
            ss_hi(1)
            v_hi(0)
            root(1)
            for t in range(2):
                act.wait_ge(s_nsqrt, t + 1)
                nc.scalar.activation(rnorm[:, t], rnorm[:, t], ACT.Ln, bias=small_eps[:, :]).then_inc(s_nln, 1)
            v_hi(1)
            for t in range(2):
                act.wait_ge(s_nln, t + 1)
                nc.scalar.activation(rnorm[:, t], rnorm[:, t], ACT.Exp, scale=-0.5).then_inc(s_r, 1)
            v_hi(2)
            v_hi(3)

            def k_hi(g):
                n, o = SIZES[g], OFFS[g]
                act.wait_ge(s_kn, g + 1)
                if g >= 1:
                    act.wait_ge(s_s, g)
                for a in range(2):
                    r = slice(64 * a, 64 * a + 64)
                    nc.scalar.activation(K[r, 0, :, a, 0:n], qk_raw[r, NP:2 * NP, o:o + n], ACT.Copy).then_inc(s_khi, 1)

            def o_hi(g):
                n = SIZES[g]
                act.wait_ge(s_pv, g + 1)
                if g >= 1:
                    act.wait_ge(s_op, g)
                for a in range(2):
                    nc.scalar.activation(oT[64 * a:64 * a + 64, 0, :, 0:n].rearrange("p (b m) n -> p b m n", b=NB),
                                         ps[64 * a:64 * a + 64, 3:6, 0:HB * n].rearrange(
                                             "p b (m a n) -> p b m a n", m=2, a=2)[:, :, :, a], ACT.Copy)\
                        .then_inc(s_ohi, 1)

            def pt_hi(g):
                n = SIZES[g]
                act.wait_ge(s_pt, g + 1)
                if g >= 1:
                    act.wait_ge(s_pv, g)
                for b in range(NB):
                    nc.scalar.activation(PT[0:n, 0, b * HB * n:(b + 1) * HB * n], ps[0:n, 3 + b, 0:HB * n],
                                         ACT.Copy).then_inc(s_pthi, 1)

            def h1_hi(g):
                n, o = SIZES[g], OFFS[g]
                act.wait_ge(s_ht1, g + 1)
                nc.scalar.activation(h1T[:, 0:2, o:o + n], ps[:, 7, 0:2 * n].rearrange("p (k n) -> p k n", k=2),
                                     ACT.Copy).then_inc(s_h1hi, 1)

            def exps(g):
                n = SIZES[g]
                act.wait_ge(s_negm, g + 1)
                if g >= 1:
                    if g >= 2:
                        act.wait_ge(s_pt, g - 1)
                    act.wait_ge(s_rinv, g)
                for h in range(H):
                    nc.scalar.activation(Pr[0:n, g % 2, h * n:(h + 1) * n], ps[0:n, h // HB, (h % HB) * n:(h % HB + 1) * n],
                                         ACT.Exp, bias=negm[0:n, h:h + 1], accum_out=psum_e[0:n, h:h + 1])\
                        .then_inc(s_e, 1)

            def w_hi_t(g):
                n, o = SIZES[g], OFFS[g]
                act.wait_ge(s_wt, g + 1)
                nc.scalar.activation(w2T[:, o:o + n], ps[0:40, 7, 256:256 + n], ACT.Copy).then_inc(s_wthi, 1)

            def expert(a, c):
                u = NT * a + c
                t = tmp[:, u % 4]
                act.wait_ge(s_g, u + 1)
                if u >= 4:
                    act.wait_ge(s_act, u - 3)
                nc.scalar.activation(t[:, 1], t[:, 0], ACT.Sigmoid, scale=ALPHA).then_inc(s_sig, 1)
                act.wait_ge(s_gu, 3 * u + 3)
                nc.scalar.activation(t[:, 2], ps[:, gu_bank(a, c, 2), 0:TH], ACT.Copy).then_inc(s_wbc, 1)
                if u >= 1:
                    act_hi(u - 1)

            def act_hi(u):
                act.wait_ge(s_act, u + 1)
                if u == NT:
                    act.wait_ge(s_pv, NG)
                nc.scalar.activation(acts[:, u // NT, u % NT, 0], tmp[:, u % 4, 4], ACT.Copy).then_inc(s_ahi, 1)

            k_hi(0)
            v_hi(4)
            v_hi(5)
            for i in range(NG + 4):
                if 2 <= i < NG + 2:
                    o_hi(i - 2)
                if 4 <= i:
                    w_hi_t(i - 4)
                if i + 1 < NG:
                    k_hi(i + 1)
                if 1 <= i <= NG:
                    pt_hi(i - 1)
                if 3 <= i < NG + 3:
                    h1_hi(i - 3)
                if i < NG:
                    exps(i)
                if i < 2 * NPAIR - 2:
                    w_hi(P_GU + 2 + i)
                if i >= NG:
                    for c in range(3 * (i - NG), 3 * (i - NG) + 3):
                        expert(0, c)
            w_hi(P_DN)
            for c in range(NT):
                expert(1, c)
                if c % 3 == 0 and c < 9:
                    w_hi(P_DN + 1 + c // 3)
            act_hi(2 * NT - 1)

        @block.vector
        def _(dve):
            def x_lo(c):
                _, n, place, dst = pieces[c]
                dve.wait_ge(*arrival(c))
                dve.wait_ge(s_xhi if c < NC else s_whi, c + 1 if c < NC else 1)
                nc.vector.tensor_tensor(dst[:, 1, :], place, f(dst[:, 0, :]), ALU.subtract)\
                    .then_inc(s_xlo if c < NC else s_w6lo, 1)
            x_lo(0)
            dve.wait_ge(s_small, 16)
            nc.vector.reciprocal(inv_scale[:, :], sm[:, C_SCALE:C_SCALE + NP]).then_inc(s_smprep, 1)
            nc.vector.tensor_scalar_add(bup1[:, :], sm[:, C_BGU:C_BGU + 2 * NT].rearrange(
                "p (s u k) -> p s u k", s=NPAIR, u=2)[:, :, 1], 1.0).then_inc(s_smprep, 1)
            dve.wait_ge(s_smhi, 1)
            nc.vector.tensor_tensor(small_lo[:, :], sm[:, C_WR:C_SMALL], f(small_hi[:, :]),
                                    ALU.subtract).then_inc(s_smlo, 1)
            nc.vector.memset(small_eps[:, :], NORM_EPS)
            nc.vector.memset(w2[:, :], 0.0)
            for c in range(1, NC + 1):
                x_lo(c)
            dve.wait_ge(s_hthi, 1)
            nc.vector.scalar_tensor_tensor(out=two(hT[:, 2]), in0=halves(4), scalar=sm[:, C_TOKB:C_TOKB + 1],
                                           in1=two(f(hT[:, 0])), op0=ALU.add, op1=ALU.subtract).then_inc(s_htlo, 1)
            dve.wait_ge(s_hthi, 2)
            up = slice(64, 128)
            nc.vector.scalar_tensor_tensor(out=two(hT[up, 1]), in0=ps[up, 6:8, 0:TH],
                                           scalar=sm[up, C_TOKB + 1:C_TOKB + 2], in1=two(f(hT[up, 1])),
                                           op0=ALU.add, op1=ALU.subtract).then_inc(s_htlo, 1)
            dve.wait_ge(s_sel, 7)
            nc.vector.tensor_copy(ident_r[:, :], ident[:, :])
            nc.vector.tensor_copy(fold_r[:, :], fold_f)
            nc.vector.tensor_copy(onehot[:, :, :], onehot_f)
            nc.vector.tensor_copy(mask_l[:, :], mask_lf)
            nc.vector.tensor_copy(mask_r[:, :], mask_rf).then_inc(s_const, 1)

            def ss_lo(t):
                dve.wait_ge(s_sshi, t + 1)
                nc.vector.tensor_tensor(ss_r[:, t, 1], ss[:, t], f(ss_r[:, t, 0]), ALU.subtract).then_inc(s_sslo, 1)

            dve.wait_ge(s_smprep, 1)
            for m in range(12):
                dve.wait_ge(s_sq, m + 1)
                if m < NP:
                    nc.vector.tensor_scalar(two(qk_raw[:, m]), halves(slot["qk", m]), inv_scale[:, m:m + 1], None,
                                            ALU.mult).then_inc(s_raw, 1)
                else:
                    nc.vector.tensor_copy(two(qk_raw[:, m]), halves(slot["qk", m])).then_inc(s_raw, 1)
                if 1 <= m < NP:
                    if m > 1:
                        dve.wait_ge(s_ssq, m - 1)
                    nc.vector.tensor_tensor(ss[:, 0], ss[:, 0], sq[:, m % 2], ALU.add).then_inc(s_ssq, 1)
                if m == 7:
                    ss_lo(0)
            ss_lo(1)

            def v_lo(g):
                n = SIZES[g]
                dve.wait_ge(s_vhi, g + 1)
                nc.vector.tensor_tensor(V[0:n, g, 1].rearrange("p (a n) -> p a n", a=2),
                                        ps[0:n, slot["v", g]:slot["v", g] + 2, 0:PD // 2],
                                        f(V[0:n, g, 0]).rearrange("p (a n) -> p a n", a=2),
                                        ALU.subtract).then_inc(s_vlo, 1)

            def q_norm(g):
                n, o = SIZES[g], OFFS[g]
                qq = qk_raw[:, 0:NP, o:o + n]
                if g == 0:
                    dve.wait_ge(s_r, 1)
                    dve.wait_ge(s_raw, NP)
                nc.vector.tensor_tensor(qq, qq, rnorm[:, 0:1, o:o + n].to_broadcast([128, NP, n]),
                                        ALU.mult).then_inc(s_qn, 1)

            def q_split(g):
                n, o = SIZES[g], OFFS[g]
                qq = qk_raw[:, 0:NP, o:o + n]
                dve.wait_ge(s_qn, g + 1)
                if g >= 1:
                    dve.wait_ge(s_s, g)
                nc.vector.tensor_copy(Q[:, 0, :, 0:n], qq).then_inc(s_qhi, 1)
                dve.wait_ge(s_qhi, g + 1)
                nc.vector.tensor_tensor(Q[:, 1, :, 0:n], qq, f(Q[:, 0, :, 0:n]),
                                        ALU.subtract).then_inc(s_qlo, 1)

            def row_max(g):
                n = SIZES[g]
                dve.wait_ge(s_s, g + 1)
                if g >= 1:
                    dve.wait_ge(s_e, H * g)
                nc.vector.reduce_max(mx[0:n, :], ps[0:n, 0:NB, 0:HB * n].rearrange("p b (h j) -> p b h j", h=HB),
                                     X).then_inc(s_mx, 1)
                dve.wait_ge(s_mx, g + 1)
                nc.vector.tensor_scalar(negm[0:n, :], mx[0:n, :], -1.0, None, ALU.mult).then_inc(s_negm, 1)

            def sum_recip(g):
                n = SIZES[g]
                dve.wait_ge(s_e, H * (g + 1))
                if g >= 1:
                    dve.wait_ge(s_p, g)
                nc.vector.reciprocal(rinv[0:n, :], psum_e[0:n, :]).then_inc(s_rinv, 1)

            def o_lo(g):
                n = SIZES[g]
                for a in range(2):
                    dve.wait_ge(s_ohi, 2 * (g + 1))
                    r = slice(64 * a, 64 * a + 64)
                    nc.vector.tensor_tensor(oT[r, 1, :, 0:n].rearrange("p (b m) n -> p b m n", b=NB),
                                            ps[r, 3:6, 0:HB * n].rearrange("p b (m a n) -> p b m a n", m=2, a=2)[:, :, :, a],
                                            f(oT[r, 0, :, 0:n]).rearrange("p (b m) n -> p b m n", b=NB),
                                            ALU.subtract).then_inc(s_olo, 1)

            def pt_lo(g):
                n = SIZES[g]
                for b in range(NB):
                    dve.wait_ge(s_pthi, NB * g + b + 1)
                    cols = slice(b * HB * n, (b + 1) * HB * n)
                    nc.vector.tensor_tensor(PT[0:n, 1, cols], ps[0:n, 3 + b, 0:HB * n], f(PT[0:n, 0, cols]),
                                            ALU.subtract).then_inc(s_ptlo, 1)

            def h1_lo(g):
                n, o = SIZES[g], OFFS[g]
                dve.wait_ge(s_h1hi, g + 1)
                nc.vector.tensor_tensor(h1T[:, 2, o:o + n], ps[:, 7, 0:n], f(h1T[:, 0, o:o + n]),
                                        ALU.subtract).then_inc(s_h1lo, 1)
                nc.vector.tensor_tensor(h1T[up, 1, o:o + n], ps[up, 7, n:2 * n], f(h1T[up, 1, o:o + n]),
                                        ALU.subtract).then_inc(s_h1lo, 1)

            def w_lo_t(g):
                n, o = SIZES[g], OFFS[g]
                dve.wait_ge(s_wthi, g + 1)
                nc.vector.tensor_tensor(w2T[32:40, o:o + n], ps[32:40, 7, 256:256 + n], f(w2T[32:40, o:o + n]),
                                        ALU.subtract).then_inc(s_wtlo, 1)

            def statistics(g, src, st_done, mv_done, ve_done):
                n = src.shape[0]
                nc.vector.bn_stats(stats[0:n, :], src).then_inc(st_done, 1)
                dve.wait_ge(st_done, g + 1)
                nc.vector.bn_aggr(mv[0:n, :], stats[0:n, :]).then_inc(mv_done, 1)
                dve.wait_ge(mv_done, g + 1)
                nc.vector.tensor_scalar_add(var_e[0:n, :], mv[0:n, 1:2], LN_EPS).then_inc(ve_done, 1)

            def ln1_stats(g):
                n = SIZES[g]
                dve.wait_ge(s_op, g + 1)
                if g >= 1:
                    dve.wait_ge(s_h1, 2 * g)
                statistics(g, ps[0:n, 6, 0:D], s_st, s_mv, s_ve)

            def ln1(g):
                n = SIZES[g]
                dve.wait_ge(s_rstd, g + 1)
                if g >= 2:
                    dve.wait_ge(s_ht1, g - 1)
                for dst, src in ((slice(0, D), slice(0, D)), (slice(D, 256), slice(DA, D))):
                    nc.vector.tensor_scalar(h1[0:n, g % 2, dst], ps[0:n, 6, src], mv[0:n, 0:1], rstd[0:n, 0:1],
                                            ALU.subtract, ALU.mult).then_inc(s_h1, 1)

            def router_top(g):
                n = SIZES[g]
                dve.wait_ge(s_rt, g + 1)
                nc.vector.tensor_tensor(lg[0:n, :], ps[0:n, 7, 384:392], sm[0:n, C_BR:C_BR + 8],
                                        ALU.add).then_inc(s_lg, 1)
                dve.wait_ge(s_lg, g + 1)
                nc.vector.max(top[0:n, :], lg[0:n, :]).then_inc(s_top, 1)
                dve.wait_ge(s_top, g + 1)
                nc.vector.tensor_tensor(rt[0:n, 2:3], top[0:n, 1:2], top[0:n, 0:1], ALU.subtract).then_inc(s_gap, 1)
                nc.vector.max_index(top_i[0:n, :], top[0:n, :], lg[0:n, :]).then_inc(s_ti, 1)
                dve.wait_ge(s_ti, 3 * g + 1)
                nc.vector.tensor_copy(rt[0:n, 0:2], top_i[0:n, 0:2]).then_inc(s_ti, 1)

            def router_weights(g):
                n = SIZES[g]
                dve.wait_ge(s_egap, g + 1)
                nc.vector.tensor_scalar_add(rt[0:n, 6:7], rt[0:n, 3:4], 1.0).then_inc(s_rs, 1)
                dve.wait_ge(s_rs, g + 1)
                nc.vector.reciprocal(rt[0:n, 4:5], rt[0:n, 6:7]).then_inc(s_p1, 1)
                dve.wait_ge(s_p1, g + 1)
                nc.vector.tensor_tensor(rt[0:n, 5:6], rt[0:n, 3:4], rt[0:n, 4:5], ALU.mult).then_inc(s_p2, 1)
                dve.wait_ge(s_ti, 3 * g + 2)
                iota = sm[0:n, C_IOTA:C_IOTA + 8]
                nc.vector.tensor_scalar(sel[0:n, 0], iota, rt[0:n, 0:1], rt[0:n, 4:5], ALU.is_equal,
                                        ALU.mult).then_inc(s_ti, 1)
                dve.wait_ge(s_p2, g + 1)
                nc.vector.tensor_scalar(sel[0:n, 1], iota, rt[0:n, 1:2], rt[0:n, 5:6], ALU.is_equal,
                                        ALU.mult).then_inc(s_sel2, 1)
                dve.wait_ge(s_sel2, g + 1)
                if g >= 1:
                    dve.wait_ge(s_wt, g)
                nc.vector.tensor_tensor(w2[0:n, 0:8], sel[0:n, 0], sel[0:n, 1], ALU.add).then_inc(s_w2, 1)
                nc.vector.tensor_tensor(w2[0:n, 32:40], sel[0:n, 0], sel[0:n, 1], ALU.add).then_inc(s_w2, 1)

            def expert_in(a, c):
                u = NT * a + c
                s, k = divmod(c, 3)
                t = tmp[:, u % 4]
                cg = C_BGU + 6 * s + k
                dve.wait_ge(s_gu, 3 * u + 1)
                if u >= 4:
                    dve.wait_ge(s_alo, u - 3)
                nc.vector.tensor_scalar(t[:, 0], ps[:, gu_bank(a, c, 0), 0:TH], sm[:, cg:cg + 1], LIMIT,
                                        ALU.add, ALU.min).then_inc(s_g, 1)
                dve.wait_ge(s_gu, 3 * u + 2)
                nc.vector.tensor_scalar(t[:, 3], ps[:, gu_bank(a, c, 1), 0:TH], bup1[:, c:c + 1], LIMIT + 1,
                                        ALU.add, ALU.min).then_inc(s_u, 1)
                if u >= 1:
                    expert_act(u - 1)
                if u >= 2:
                    expert_lo(u - 2)

            def expert_act(u):
                t = tmp[:, u % 4]
                dve.wait_ge(s_glw, u + 1)
                dve.wait_ge(s_u, u + 1)
                nc.vector.scalar_tensor_tensor(out=t[:, 4], in0=t[:, 3], scalar=1.0 - LIMIT, in1=t[:, 1],
                                               op0=ALU.max, op1=ALU.mult).then_inc(s_act, 1)

            def expert_lo(u):
                dve.wait_ge(s_ahi, u + 1)
                a, c = divmod(u, NT)
                nc.vector.tensor_tensor(acts[:, a, c, 1], tmp[:, u % 4, 4], f(acts[:, a, c, 0]),
                                        ALU.subtract).then_inc(s_alo, 1)

            def ln2(j):
                tile = ps[0:TD, down_bank(j), 0:D]
                dve.wait_ge(s_dn, j + 1)
                statistics(j, tile, s_zst, s_zmv, s_zve)
                dve.wait_ge(s_zrstd, j + 1)
                if j >= 2:
                    dve.wait_ge(s_out[j % 2], 16 * (j // 2))
                nc.vector.tensor_scalar(res[0:TD, j % 2, :], tile, mv[0:TD, 0:1], rstd[0:TD, 0:1],
                                        ALU.subtract, ALU.mult).then_inc(s_res, 1)

            v_lo(0)
            v_lo(1)
            q_norm(0)
            q_split(0)
            for g in range(2, NG):
                v_lo(g)
            for i in range(NG + 4):
                if 1 <= i <= NG:
                    sum_recip(i - 1)
                if 2 <= i < NG + 2:
                    o_lo(i - 2)
                if i + 1 < NG:
                    q_norm(i + 1)
                if i < NG:
                    row_max(i)
                if 4 <= i:
                    w_lo_t(i - 4)
                if i + 1 < NG:
                    q_split(i + 1)
                if 3 <= i < NG + 3:
                    h1_lo(i - 3)
                if 1 <= i <= NG:
                    pt_lo(i - 1)
                if 2 <= i < NG + 2:
                    ln1_stats(i - 2)
                if 3 <= i < NG + 3:
                    router_top(i - 3)
                if 2 <= i < NG + 2:
                    ln1(i - 2)
                if 3 <= i < NG + 3:
                    router_weights(i - 3)
                if i >= NG:
                    for c in range(3 * (i - NG), 3 * (i - NG) + 3):
                        expert_in(0, c)
            for c in range(NT):
                expert_in(1, c)
            expert_act(2 * NT - 1)
            expert_lo(2 * NT - 2)
            expert_lo(2 * NT - 1)
            for j in range(ND):
                ln2(j)

        @block.tensor
        def _(pe):
            mm = nc.tensor.matmul

            for c in range(NC):
                pe.wait_ge(s_xlo, c + 1)
                hi, lo = xw[:, c, 0], xw[:, c, 1]
                for wx, px in ((hi, hi), (hi, lo), (lo, hi)):
                    for t in range(2):
                        for a in range(2):
                            last = mm(ps[:, 4 + 2 * t + a, 0:TH], wx[:, T + 128 * t:T + 128 * t + 128],
                                      px[:, TH * a:TH * a + TH], start=(c == 0 and wx is hi and px is hi),
                                      stop=(c == NC - 1 and wx is lo))
                last.then_inc(s_tok, 1)

            def wide(bank, w_a, w_b, x, a):
                cols = slice(TH * a, TH * a + TH)
                out_ap = ps[:, bank, 0:TH]
                mm(out_ap, w_a(0), x[:, 0, cols], start=True, stop=False)
                mm(out_ap, w_a(1), x[:, 0, cols], start=False, stop=False)
                mm(out_ap, w_a(0), x[:, 2, cols], start=False, stop=False)
                mm(out_ap, w_b(0), x[:, 1, cols], start=False, stop=False)
                return mm(out_ap, w_b(1), x[:, 1, cols], start=False, stop=True)

            def norm_sum(t):
                pe.wait_ge(s_sslo, t + 1)
                pe.wait_ge(*slot_read(("sum", t)))
                for a in range(2):
                    for k in range(2):
                        last = mm(ps[:, slot["sum", t] + a, 0:TH], fold_r[:, :], ss_r[:, t, k, TH * a:TH * a + TH],
                                  start=(k == 0), stop=(k == 1))
                last.then_inc(s_nsum, 1)

            pe.wait_ge(s_htlo, 2)
            pe.wait_ge(s_const, 1)
            for m in range(12):
                s, p = divmod(m, NP)
                if m == 0:
                    pe.wait_ge(s_w6lo, 1)
                pe.wait_ge(s_wlo, w_ready(P_QKV + 2 * s + 1))
                if slot_read(("qk", m)):
                    pe.wait_ge(*slot_read(("qk", m)))
                cols = slice(128 * p, 128 * p + 128)
                for a in range(2):
                    last = wide(slot["qk", m] + a, lambda k: wqkv[:, s, 0, k, cols],
                                lambda k: wqkv[:, s, 1, k, cols], hT, a)
                last.then_inc(s_qk, 1)
                if m == 10:
                    norm_sum(0)

            def v_proj(g):
                n, o = SIZES[g], OFFS[g]
                if g == 0:
                    pe.wait_ge(s_wlo, w_ready(P_QKV + 5))
                pe.wait_ge(*slot_read(("v", g)))
                tok = slice(o, o + n)
                for a in range(2):
                    cols = slice(PD // 2 * a, PD // 2 * (a + 1))
                    out_ap = ps[0:n, slot["v", g] + a, 0:PD // 2]
                    mm(out_ap, hT[:, 0, tok], wqkv[:, 2, 0, 0, cols], start=True, stop=False)
                    mm(out_ap, hT[:, 0, tok], wqkv[:, 2, 0, 1, cols], start=False, stop=False)
                    mm(out_ap, hT[:, 2, tok], wqkv[:, 2, 0, 0, cols], start=False, stop=False)
                    mm(out_ap, hT[:, 1, tok], wqkv[:, 2, 1, 0, cols], start=False, stop=False)
                    last = mm(out_ap, hT[:, 1, tok], wqkv[:, 2, 1, 1, cols], start=False, stop=True)
                last.then_inc(s_v, 1)

            v_proj(0)
            norm_sum(1)
            for g in range(1, NG):
                v_proj(g)

            def scores(g):
                n = SIZES[g]
                pe.wait_ge(s_qlo, g + 1)
                pe.wait_ge(s_klo, 2 * (g + 1))
                if g == 0:
                    pe.wait_ge(s_vlo, NG)
                for b in range(NB):
                    if g >= 1:
                        pe.wait_ge(s_e, H * (g - 1) + HB * (b + 1))
                    mm(ps[0:n, b, 0:HB * n], mask_l[:, 0:n],
                       mask_r[:, :].rearrange("p (h j) -> p h j", h=HB)[:, :, 0:n], start=True, stop=False,
                       skip_group_check=True)
                    for j in range(2):
                        m = 2 * b + j
                        for qp, kp in ((0, 0), (0, 1), (1, 0)):
                            last = mm(ps[0:n, b, 2 * n * j:2 * n * (j + 1)], Q[:, qp, m, 0:n], K[:, kp, m, :, 0:n],
                                      start=False, stop=(qp == 1), skip_group_check=True)
                last.then_inc(s_s, 1)

            def p_transpose(g):
                n = SIZES[g]
                pe.wait_ge(s_p, g + 1)
                if g >= 1:
                    pe.wait_ge(s_olo, 2 * g)
                for h in range(H):
                    last = nc.tensor.transpose(ps[0:n, 3 + h // HB, (h % HB) * n:(h % HB + 1) * n],
                                               Pr[0:n, g % 2, h * n:(h + 1) * n], ident[0:n, 0:n])
                last.then_inc(s_pt, 1)

            def weighted(g):
                n = SIZES[g]
                for p in range(NP):
                    b = p // 2
                    pe.wait_ge(s_ptlo, NB * g + b + 1)
                    pe.wait_ge(s_vlo, g + 1)
                    out_ap = ps[:, 3 + b, (p % 2) * 2 * n:(p % 2 + 1) * 2 * n]
                    for vp, pp in ((0, 0), (0, 1), (1, 0)):
                        last = mm(out_ap, V[0:n, g, vp, 128 * p:128 * p + 128], PT[0:n, pp, 2 * p * n:2 * (p + 1) * n],
                                  start=(vp == 0 and pp == 0), stop=(vp == 1))
                last.then_inc(s_pv, 1)

            def project(g):
                n, o = SIZES[g], OFFS[g]
                pe.wait_ge(s_olo, 2 * (g + 1))
                pe.wait_ge(s_wlo, w_ready(P_OUT + 1))
                if g >= 1:
                    pe.wait_ge(s_h1, 2 * g)
                tok = slice(o, o + n)
                for p in range(NP):
                    for op_, wp in ((0, 0), (0, 1), (1, 0)):
                        mm(ps[0:n, 6, 0:D], oT[:, op_, p, 0:n], wout[:, p // 3, wp, p % 3, :],
                           start=(p == 0 and op_ == 0 and wp == 0), stop=False)
                pick = ident_r[:, BOUT_ROW:BOUT_ROW + 1].to_broadcast([128, n])
                mm(ps[0:n, 6, 0:D], pick, small_hi[:, 16:16 + D], start=False, stop=False)
                mm(ps[0:n, 6, 0:D], pick, small_lo[:, 16:16 + D], start=False, stop=False)
                residual(ps[0:n, 6], hT, tok, True).then_inc(s_op, 1)

            def residual(bank, x, tok, stop):
                mm(bank[:, 0:DA], x[:, 0, tok], ident_r[:, :], start=False, stop=False)
                mm(bank[:, 0:DA], x[:, 2, tok], ident_r[:, :], start=False, stop=False)
                return mm(bank[:, DA:D], x[:, 1, tok], fold_r[:, 0:DB], start=False, stop=stop)

            def h1_transpose(g):
                n = SIZES[g]
                pe.wait_ge(s_h1, 2 * (g + 1))
                if g >= 1:
                    pe.wait_ge(s_wtlo, g)
                for k in range(2):
                    last = nc.tensor.transpose(ps[:, 7, k * n:(k + 1) * n], h1[0:n, g % 2, 128 * k:128 * k + 128],
                                               ident[0:n, 0:n])
                last.then_inc(s_ht1, 1)

            def logits(g):
                n, o = SIZES[g], OFFS[g]
                tok = slice(o, o + n)
                pe.wait_ge(s_h1lo, 2 * (g + 1))
                out_ap = ps[0:n, 7, 384:392]
                a_hi, a_lo, b_hi, b_lo = small_hi[:, 0:8], small_lo[:, 0:8], small_hi[:, 8:16], small_lo[:, 8:16]
                mm(out_ap, h1T[:, 0, tok], a_hi, start=True, stop=False)
                mm(out_ap, h1T[:, 0, tok], a_lo, start=False, stop=False)
                mm(out_ap, h1T[:, 2, tok], a_hi, start=False, stop=False)
                mm(out_ap, h1T[:, 1, tok], b_hi, start=False, stop=False)
                mm(out_ap, h1T[:, 1, tok], b_lo, start=False, stop=True).then_inc(s_rt, 1)

            def w_transpose(g):
                n = SIZES[g]
                pe.wait_ge(s_w2, 2 * (g + 1))
                nc.tensor.transpose(ps[0:40, 7, 256:256 + n], w2[0:n, :], ident[0:n, 0:n]).then_inc(s_wt, 1)

            def expert(a, c):
                n = NT * a + c
                s, k = divmod(c, 3)
                if n == 0:
                    pe.wait_ge(s_e, H * NG)
                if c == 0:
                    pe.wait_ge(s_wtlo, 3 if a == 0 else NG)
                if a == 0:
                    pe.wait_ge(s_wlo, w_ready(P_GU + 2 * GU_ORDER.index(s) + 1))
                for u in range(3):
                    back = 2 if u < 2 and n >= NT + 2 else 1
                    if n == NT + 1 and u < 2:
                        pe.wait_ge(s_h1, 2 * NG)
                    elif n >= back:
                        pe.wait_ge((s_g, s_u, s_wbc)[u], n - back + 1)
                    bank = gu_bank(a, c, u)
                    if u < 2:
                        cols = slice(384 * u + 128 * k, 384 * u + 128 * k + 128)
                        last = wide(bank, lambda j: wgu[:, s, 0, j, cols], lambda j: wgu[:, s, 1, j, cols], h1T, a)
                    else:
                        first = 256 * s + (0, 128, 64)[k]
                        w = onehot[:, :, :].rearrange("p e n -> p (e n)")[:, first:first + 128]
                        last = mm(ps[:, bank, 0:TH], w, w2T[:, TH * a:TH * a + TH], start=True, stop=True)
                    last.then_inc(s_gu, 1)

            def down_bias(j):
                tok = slice(TD * j, TD * j + TD)
                bank = ps[0:TD, down_bank(j)]
                mm(bank[:, 0:D], w2T[:, tok], small_hi[0:40, 16:16 + D], start=True, stop=False)
                mm(bank[:, 0:D], w2T[:, tok], small_lo[0:40, 16:16 + D], start=False, stop=False)
                residual(bank, h1T, tok, False)

            def down(j, c):
                a, jj = divmod(j, ND // 2)
                tok = slice(TD * jj, TD * jj + TD)
                pe.wait_ge(s_alo, NT * a + c + 1)
                pe.wait_ge(s_wlo, w_ready(P_DN + c // 3))
                for ap_, wp in ((0, 0), (0, 1), (1, 0)):
                    last = mm(ps[0:TD, down_bank(j), 0:D], acts[:, a, c, ap_, tok], wd[:, c // 3, wp, c % 3],
                              start=False, stop=(c == NT - 1 and ap_ == 1))
                return last

            pe.wait_ge(s_smlo, 1)
            for i in range(NG + 4):
                if i < NG:
                    scores(i)
                if 4 <= i:
                    w_transpose(i - 4)
                if 1 <= i <= NG:
                    p_transpose(i - 1)
                if 3 <= i < NG + 3:
                    h1_transpose(i - 3)
                if 2 <= i < NG + 2:
                    project(i - 2)
                if 3 <= i < NG + 3:
                    logits(i - 3)
                if 1 <= i <= NG:
                    weighted(i - 1)

                if i >= NG:
                    for c in range(3 * (i - NG), 3 * (i - NG) + 3):
                        expert(0, c)
            for c in range(NT):
                expert(1, c)
                if c == 0:
                    pe.wait_ge(s_olo, 2 * NG)
                    for j in range(ND // 2):
                        down_bias(j)
                for j in range(ND // 2):
                    last = down(j, c)
                    if c == NT - 1:
                        last.then_inc(s_dn, 1)
            pe.wait_ge(s_g, 2 * NT)
            pe.wait_ge(s_u, 2 * NT)
            pe.wait_ge(s_wbc, 2 * NT)
            for j in range(ND // 2, ND):
                down_bias(j)
                for c in range(NT):
                    last = down(j, c)
                last.then_inc(s_dn, 1)


def kernel(x, L0_tok_W, L0_tok_b, L0_attn_w_qkv, L0_attn_w_out, L0_attn_b_out, L0_attn_scale, L0_ffn_Wr, L0_ffn_br,
           L0_ffn_Wgu, L0_ffn_bgu, L0_ffn_Wd, L0_ffn_bd):
    import numpy as np
    import concourse.bacc as bacc
    from concourse.bass_utils import run_bass_kernel_spmd

    def arr(a):
        return np.asarray(a)

    p = 16
    xT = arr(x).reshape(B, 6, p, 6, p, 3).transpose(2, 4, 5, 0, 1, 3).reshape(NC, 128, T)
    w_tok = arr(L0_tok_W).reshape(NC, 128, D)
    w_tok = np.concatenate([w_tok, w_tok[:, :, DA:]], axis=2)
    wqkvT = arr(L0_attn_w_qkv).T.reshape(D, 3, PD).transpose(1, 0, 2)
    w_outT = arr(L0_attn_w_out).T.reshape(NC, 128, D).reshape(2, 3, 128, D).transpose(0, 2, 1, 3)\
        .reshape(2, 128, 3 * D)

    def tiles(a):
        lead = a.shape[0]
        a = a.reshape(lead, NPAIR, 2, 2, FI)
        full = a[..., :DA].transpose(0, 1, 3, 2, 4).reshape(lead, NPAIR, 2, 2 * DA)
        rest = a[..., DA:].transpose(0, 1, 3, 2, 4).reshape(lead, NPAIR, 2, 2 * DB)
        return np.concatenate([full, rest], axis=3).reshape(lead, NPAIR, 6 * 128)
    w_gu = tiles(arr(L0_ffn_Wgu).transpose(1, 0, 2).reshape(D, E * 2 * FI)).transpose(1, 0, 2)
    b_gu = tiles(arr(L0_ffn_bgu).reshape(1, E * 2 * FI)).reshape(NPAIR * 6, 128).T
    wd = arr(L0_ffn_Wd).reshape(NPAIR, 2, FI, D)
    wd = np.concatenate([wd[:, :, :DA].reshape(NPAIR, 2 * DA, D), wd[:, :, DA:].reshape(NPAIR, 2 * DB, D)], axis=1)
    wd = wd.reshape(4, 3, 128, D).transpose(0, 2, 1, 3).reshape(4, 128, 3 * D)

    small = np.zeros((128, C_SMALL), np.float32)
    tok_b = arr(L0_tok_b)
    small[:, C_TOKB] = tok_b[:DA]
    small[:DB, C_TOKB + 1] = small[DB:, C_TOKB + 1] = tok_b[DA:]
    small[:, C_SCALE:C_SCALE + NP] = np.repeat(arr(L0_attn_scale).reshape(NP, 2).T, DH, axis=0)
    small[:, C_BR:C_BR + E] = arr(L0_ffn_br)
    small[:, C_BGU:C_BGU + 2 * NT] = b_gu
    small[:, C_IOTA:C_IOTA + E] = np.arange(E)
    small[BOUT_ROW, C_BD:C_BD + D] = arr(L0_attn_b_out)
    small[:, C_WR:C_WR + E] = arr(L0_ffn_Wr)[:DA]
    small[:DB, C_WR + E:C_WR + 2 * E] = small[DB:, C_WR + E:C_WR + 2 * E] = arr(L0_ffn_Wr)[DA:]
    small[0:E, C_BD:C_BD + D] = small[32:32 + E, C_BD:C_BD + D] = arr(L0_ffn_bd)

    ins = {"xT": xT, "w_tok": w_tok, "w_qkv_a": wqkvT[:, :DA], "w_qkv_b": wqkvT[:, DA:], "w_out": w_outT,
           "w_gu_a": w_gu[:, :DA], "w_gu_b": w_gu[:, DA:], "w_down": wd, "small": small}
    nc = bacc.Bacc("TRN2", target_bir_lowering=False, num_devices=1)
    arrays, aps = {}, []
    for name, a in ins.items():
        arrays[name] = np.ascontiguousarray(a)
        aps.append(nc.dram_tensor(name, a.shape, mybir.dt.float32, kind="ExternalInput").ap())
    out = nc.dram_tensor("out", (T, D), mybir.dt.float32, kind="ExternalOutput").ap()
    vit_layer(nc, *aps, out)
    r = run_bass_kernel_spmd(nc, [arrays], core_ids=[0])
    return r.results[0]["out"].reshape(B, SEQ, D)
```

```python
import math

import concourse.bass as bass
from concourse import mybir
from contextlib import ExitStack


D = 192
DA, DB = 128, 64
PD, NC = 768, 6
B, SEQ = 16, 36
T = B * SEQ
TH = T // 2
H, DH = 12, 64
NP = H // 2
E, FI = 8, 192
NPAIR = E // 2
NT = 3 * NPAIR
IMG = 3
GRP = IMG * SEQ
SIZES = [GRP] * (B // IMG) + [SEQ * (B % IMG)] * (B % IMG > 0)
GU_ORDER = [3, 0, 1, 2]
OFFS = [GRP * g for g in range(len(SIZES))]
NG = len(SIZES)
BANK = 512
HB = 4
NB = H // HB
LN_EPS, NORM_EPS = 1e-5, 1e-8
ALPHA, LIMIT = 1.702, 7.0
MASKED = -2.0 ** 126

C_TOKB, C_SCALE, C_BR, C_BGU, C_IOTA, C_WR, C_BD = 0, 2, 8, 16, 40, 48, 64
C_SMALL = C_BD + D
BOUT_ROW = 64

STG = 4
STGW = 768
XW = T + 2 * 128
TD = 96
ND = T // TD


def vit_layer(nc, xT, w_tok, w_qkv_a, w_qkv_b, w_out, w_gu_a, w_gu_b, w_down, small, out):
    f32, f32r, bf16, u32 = mybir.dt.float32, mybir.dt.float32r, mybir.dt.bfloat16, mybir.dt.uint32
    ALU = mybir.AluOpType
    ACT = mybir.ActivationFunctionType
    X = mybir.AxisListType.X

    ctx = ExitStack()
    with ctx:
        def sb(name, shape, dt=f32):
            return ctx.enter_context(nc.sbuf_tensor(name, shape, dt))

        def sem(name):
            return ctx.enter_context(nc.semaphore(name))

        def f(ap):
            return ap.bitcast(f32)

        reg_a = sb("reg_a", [128, 15696], f32r)
        reg_b = sb("reg_b", [128, 12288], f32r)
        reg_c = sb("reg_c", [128, 5328], f32r)
        h1T = sb("h1T", [128, 3, T], f32r)
        w2T = sb("w2T", [40, T], f32r)
        onehot = sb("onehot", [40, E, 128], f32r)
        ident_r = sb("ident_r", [128, 128], f32r)
        minus_r = sb("minus_r", [128, 128], f32r)
        fold_r = sb("fold_r", [128, 128], f32r)
        small_hi = sb("small_hi", [128, 16 + D], f32r)
        small_lo = sb("small_lo", [128, 16 + D], f32r)
        filler = sb("filler", [128, BANK], bf16)
        mask_l = sb("mask_l", [128, GRP], bf16)
        mask_r = sb("mask_r", [128, HB * GRP], bf16)

        xw = reg_a[:, 0:NC * 2 * XW].rearrange("p (s k n) -> p s k n", s=NC, k=2)
        V = reg_a[:, 0:NG * 2 * PD].rearrange("p (g k n) -> p g k n", g=NG, k=2)
        Q = reg_a[:, 9216:9216 + 2 * NP * GRP].rearrange("p (k m n) -> p k m n", k=2, m=NP)
        K = reg_a[:, 10512:10512 + 4 * NP * GRP].rearrange("p (k m a n) -> p k m a n", k=2, m=NP, a=2)
        PT = reg_a[:, 13104:13104 + 2 * H * GRP].rearrange("p (k n) -> p k n", k=2)
        acts = reg_a[:, 0:2 * NT * T].rearrange("p (a c k n) -> p a c k n", a=2, c=NT, k=2)
        wqkv = reg_b[:, 0:4 * 3 * PD].rearrange("p (s c k n) -> p s c k n", s=3, c=2, k=2)
        wgu = reg_b[:, :].rearrange("p (s c k n) -> p s c k n", s=NPAIR, c=2, k=2)
        wout = reg_c[:, 0:2 * NC * D].rearrange("p (s k c n) -> p s k c n", s=2, k=2, c=3)
        hT = reg_c[:, 2304:2304 + 3 * T].rearrange("p (k n) -> p k n", k=3)
        oT = reg_c[:, 4032:4032 + 2 * NP * GRP].rearrange("p (k m n) -> p k m n", k=2, m=NP)
        wd = reg_c[:, 0:2 * NT * D].rearrange("p (s k c n) -> p s k c n", s=4, k=2, c=3)

        stage = sb("stage", [128, STG, STGW])
        reg_q = sb("reg_q", [128, 12 * T])
        qk_raw = reg_q[:, :].rearrange("p (m n) -> p m n", m=12)
        xstage = reg_q[:, 0:NC * XW].rearrange("p (c n) -> p c n", c=NC)
        tmp = reg_q[:, :].rearrange("p (s k n) -> p s k n", s=4, k=6)
        rnorm = sb("rnorm", [128, 2, T])
        Pr = sb("Pr", [128, 2, H * GRP])
        h1 = sb("h1", [128, 2, 256])
        sq = Pr[:, 0, 0:2 * T].rearrange("p (k n) -> p k n", k=2)
        ss = Pr[:, 1, 0:2 * T].rearrange("p (k n) -> p k n", k=2)
        ss_r = reg_a[:, 13104:13104 + 4 * T].rearrange("p (t k n) -> p t k n", t=2, k=2)
        sm = sb("sm", [128, C_SMALL])
        inv_scale = sb("inv_scale", [128, NP])
        bup1 = sb("bup1", [128, NT])
        small_eps = sb("small_eps", [128, 1])
        ident = sb("ident", [128, 128])
        half = sb("half", [128, 1])
        euler = sb("euler", [128, 1])
        mx_r = sb("mx_r", [128, H], f32r)
        psum_e = sb("psum_e", [128, H])
        rinv = sb("rinv", [128, H])
        stats = sb("stats", [128, 6])
        mv = sb("mv", [128, 2])
        var_e = sb("var_e", [128, 1])
        rstd = sb("rstd", [128, 1])
        lg = sb("lg", [128, 8])
        top = sb("top", [128, 8])
        top_i = sb("top_i", [128, 8], u32)
        rt = sb("rt", [128, 8])
        sel = sb("sel", [128, 2, 8])
        w2 = sb("w2", [128, 40])
        res = rnorm[:, 1, 0:2 * D].rearrange("p (k n) -> p k n", k=2)
        onehot_f = Pr[0:40, 0, 0:E * 128].rearrange("p (e n) -> p e n", e=E)
        fold_f = rnorm[:, 0, 0:128]
        mask_lf = rnorm[:, 0, 128:128 + GRP]
        mask_rf = rnorm[:, 1, 0:HB * GRP]

        ps = ctx.enter_context(nc.psum_tensor("ps", [128, 8, BANK], f32))

        def halves(bank):
            return ps[:, bank:bank + 2, 0:TH]

        def two(ap):
            return ap.rearrange("p (a n) -> p a n", a=2)

        s_stage = [sem(f"s_stage{i}") for i in range(STG)]
        s_xst = [sem(f"s_xst{i}") for i in range(NC)]
        s_small = sem("s_small")
        s_out = [sem(f"s_out{i}") for i in range(2)]
        (s_filler, s_fill, s_sel, s_const, s_smprep, s_smhi, s_smlo, s_xhi, s_xlo, s_whi, s_wlo, s_w6lo, s_tok, s_hthi, s_htlo,
         s_qk, s_raw, s_sq, s_ssq, s_ssk, s_sshi, s_sslo, s_nsum, s_nsqrt, s_nln, s_r, s_v, s_vhi, s_vlo,
         s_qn, s_kn, s_kn0, s_klo0, s_eps0, s_rec0, s_r0, s_qhi, s_qlo, s_khi, s_klo, s_s, s_mx, s_sub, s_e, s_rinv, s_p, s_pt, s_pthi, s_ptlo, s_pv,
         s_ohi, s_olo, s_op, s_st, s_mv, s_ve, s_rstd, s_h1, s_ht1, s_h1hi, s_h1lo, s_rt, s_lg, s_top, s_ti,
         s_gap, s_egap, s_rs, s_p1, s_p2, s_sel2, s_w2, s_wt, s_wthi, s_wtlo, s_gu, s_g, s_sig, s_glu, s_wbc,
         s_glw, s_u, s_act, s_ahi, s_alo, s_dn, s_zst, s_zmv, s_zve, s_zrstd, s_res) = [
            sem(n) for n in (
                "s_filler s_fill s_sel s_const s_smprep s_smhi s_smlo s_xhi s_xlo s_whi s_wlo s_w6lo s_tok s_hthi s_htlo "
                "s_qk s_raw s_sq s_ssq s_ssk s_sshi s_sslo s_nsum s_nsqrt s_nln s_r s_v s_vhi s_vlo "
                "s_qn s_kn s_kn0 s_klo0 s_eps0 s_rec0 s_r0 s_qhi s_qlo s_khi s_klo s_s s_mx s_sub s_e s_rinv s_p s_pt s_pthi s_ptlo s_pv "
                "s_ohi s_olo s_op s_st s_mv s_ve s_rstd s_h1 s_ht1 s_h1hi s_h1lo s_rt s_lg s_top s_ti "
                "s_gap s_egap s_rs s_p1 s_p2 s_sel2 s_w2 s_wt s_wthi s_wtlo s_gu s_g s_sig s_glu s_wbc "
                "s_glw s_u s_act s_ahi s_alo s_dn s_zst s_zmv s_zve s_zrstd s_res").split()]

        pieces = []
        for c in range(NC):
            pieces.append(([(xT[c], 0, 128, 0, T), (w_tok[c], 0, 128, T, 256)], XW, xstage[:, c], xw[:, c]))

        def add_weight(loads, n, dst):
            pieces.append((loads, n, stage[:, (len(pieces) - NC) % STG, 0:n], dst))
        for s in range(3):
            add_weight([(w_qkv_a[s], 0, 128, 0, PD)], PD, wqkv[:, s, 0])
            add_weight([(w_qkv_b[s], 0, 64, 0, PD), (w_qkv_b[s], 64, 128, 0, PD)], PD, wqkv[:, s, 1])
        for s in range(2):
            add_weight([(w_out[s], 0, 128, 0, 3 * D)], 3 * D, wout[:, s].rearrange("p k c n -> p k (c n)"))
        for s in GU_ORDER:
            add_weight([(w_gu_a[s], 0, 128, 0, 768)], 768, wgu[:, s, 0])
            add_weight([(w_gu_b[s], 0, 64, 0, 768), (w_gu_b[s], 64, 128, 0, 768)], 768, wgu[:, s, 1])
        for s in range(4):
            add_weight([(w_down[s], 0, 128, 0, 3 * D)], 3 * D, wd[:, s].rearrange("p k c n -> p k (c n)"))
        P_QKV, P_OUT = NC, NC + 6
        P_GU = P_OUT + 2
        P_DN = P_GU + 2 * NPAIR
        arrived = []
        for k, (loads, _, _, _) in enumerate(pieces):
            arrived.append(16 * len(loads) + (arrived[k - STG] if k >= NC + STG else 0))

        def arrival(k):
            return (s_xst[k] if k < NC else s_stage[(k - NC) % STG]), arrived[k]

        def w_ready(k):
            return k - NC

        uses = [("qk", m) for m in range(11)] + [("sum", 0), ("qk", 11), ("v", 0), ("v", 1), ("v", 2), ("sum", 1)]
        uses += [("v", g) for g in range(3, NG)]
        slot = {use: 2 * (n % 4) for n, use in enumerate(uses)}

        def slot_read(use):
            n = uses.index(use)
            if n < 4:
                return None
            kind, j = uses[n - 4]
            return {"qk": s_raw, "sum": s_nsqrt, "v": s_vlo}[kind], j + 1

        def down_bank(j):
            return 3 + j if j < ND // 2 else j - ND // 2

        def gu_bank(a, c, u):
            return 6 + u if a == 1 and c % 2 and u < 2 else u

        block = ctx.enter_context(nc.Block())

        @block.sync
        def _(sp):
            for k, (loads, _, place, _) in enumerate(pieces):
                if k == NC + STG:
                    sp.wait_ge(s_w6lo, 1)
                elif k > NC + STG:
                    sp.wait_ge(s_wlo, w_ready(k - STG))
                for src, p0, p1, c0, n in loads:
                    sp.dma_start(place[p0:p1, c0:c0 + n], src).then_inc(arrival(k)[0], 16)
                if k == 0:
                    sp.dma_start(sm[:, :], small).then_inc(s_small, 16)
            for j in range(ND):
                sp.wait_ge(s_res, j + 1)
                sp.dma_start(out[TD * j:TD * j + TD, :], res[0:TD, j % 2, :]).then_inc(s_out[j % 2], 16)
            for i in range(2):
                sp.wait_ge(s_out[i], 16 * (ND // 2))

        @block.gpsimd
        def _(pool):
            nc.gpsimd.memset(filler[:, :], 0.0).then_inc(s_filler, 1)
            for t, value in ((ident[:, :], 0.0), (fold_f, 0.0), (onehot_f, 0.0), (mask_lf, 0.0), (half[:, :], -0.5),
                             (euler[:, :], math.e)):
                nc.gpsimd.memset(t, value).then_inc(s_fill, 1)
            nc.gpsimd.memset(mask_rf, MASKED).then_inc(s_fill, 1)
            pool.wait_ge(s_fill, 7)
            nc.gpsimd.memset(f(K[64:128, :, :, 0]), 0.0).then_inc(s_fill, 1)
            pool.wait_ge(s_fill, 8)
            nc.gpsimd.memset(f(K[0:64, :, :, 1]), 0.0).then_inc(s_fill, 1)
            pool.wait_ge(s_fill, 9)

            def fill(ap, base, pattern, value, n):
                pool.wait_ge(s_sel, n)
                nc.gpsimd.affine_select(out=ap, in_=ap, compare_op=ALU.not_equal, fill=value, base=base,
                                        pattern=pattern, channel_multiplier=1).then_inc(s_sel, 1)
            nc.gpsimd.affine_select(out=ident[:, :], in_=ident[:, :], compare_op=ALU.not_equal, fill=1.0, base=0,
                                    pattern=[[-1, 128]], channel_multiplier=1).then_inc(s_sel, 1)
            fold3 = fold_f.rearrange("p (a n) -> p a n", a=2)
            fill(fold3, 0, [[0, 2], [-1, 64]], 1.0, 1)
            fill(fold3, -64, [[0, 2], [-1, 64]], 1.0, 2)
            fill(mask_lf.rearrange("p (a n) -> p a n", a=IMG), 0, [[-1, IMG], [0, SEQ]], 1.0, 3)
            fill(mask_rf.rearrange("p (h a n) -> p h a n", h=HB, a=IMG), 0, [[0, HB], [-1, IMG], [0, SEQ]], 0.0, 4)
            fill(onehot_f, 0, [[-1, E], [0, 128]], 1.0, 5)
            fill(onehot_f, -32, [[-1, E], [0, 128]], 1.0, 6)

            def w_lo(k):
                _, n, place, dst = pieces[k]
                pool.wait_ge(*arrival(k))
                pool.wait_ge(s_whi, w_ready(k) + 1)
                if P_GU + 2 <= k:
                    pool.wait_ge(s_v, NG)
                if P_DN <= k:
                    pool.wait_ge(s_op, NG)
                nc.gpsimd.tensor_tensor(dst[:, 1, :], place, f(dst[:, 0, :]), ALU.subtract).then_inc(s_wlo, 1)
            for k in range(P_QKV + 1, P_QKV + 6):
                w_lo(k)
            for m in range(7, 12):
                pool.wait_ge(s_sq, m + 1)
                if m > 7:
                    pool.wait_ge(s_ssk, m - 7)
                nc.gpsimd.tensor_tensor(ss[:, 1], ss[:, 1], sq[:, m % 2], ALU.add).then_inc(s_ssk, 1)
            for k in range(P_OUT, P_GU + 2):
                w_lo(k)

            def k_norm(g):
                n, o = SIZES[g], OFFS[g]
                kk = qk_raw[:, NP:2 * NP, o:o + n]
                if g == 1:
                    pool.wait_ge(s_r, 2)
                    pool.wait_ge(s_raw, 12)
                nc.gpsimd.tensor_tensor(kk, kk, rnorm[:, 1:2, o:o + n].to_broadcast([128, NP, n]),
                                        ALU.mult).then_inc(s_kn, 1)

            def k_lo(g):
                n, o = SIZES[g], OFFS[g]
                pool.wait_ge(s_kn, g)
                pool.wait_ge(s_khi, 2 * (g + 1))
                pool.wait_ge(s_s, g)
                for a in range(2):
                    r = slice(64 * a, 64 * a + 64)
                    if a == 1:
                        pool.wait_ge(s_klo, 2 * g - 1)
                    nc.gpsimd.tensor_tensor(K[r, 1, :, a, 0:n], qk_raw[r, NP:2 * NP, o:o + n], f(K[r, 0, :, a, 0:n]),
                                            ALU.subtract).then_inc(s_klo, 1)
                pool.wait_ge(s_klo, 2 * g)

            def probs(g):
                n = SIZES[g]
                pool.wait_ge(s_rinv, g + 1)
                pool.wait_ge(s_e, H * (g + 1))
                pp = Pr[0:n, g % 2, 0:H * n].rearrange("p (h j) -> p h j", h=H)
                nc.gpsimd.tensor_tensor(pp, pp, rinv[0:n, :].unsqueeze(2).to_broadcast([n, H, n]),
                                        ALU.mult).then_inc(s_p, 1)

            def root(g, n, ve, done):
                pool.wait_ge(ve, g + 1)
                nc.gpsimd.tensor_tensor(rstd[0:n, :], var_e[0:n, :], half[0:n, :], ALU.pow).then_inc(done, 1)

            def gap_exp(g):
                n = SIZES[g]
                pool.wait_ge(s_gap, g + 1)
                nc.gpsimd.tensor_tensor(rt[0:n, 3:4], euler[0:n, :], rt[0:n, 2:3], ALU.pow).then_inc(s_egap, 1)

            def expert(a, c):
                u = NT * a + c
                t = tmp[:, u % 4]
                pool.wait_ge(s_g, u + 1)
                pool.wait_ge(s_sig, u + 1)
                nc.gpsimd.tensor_tensor(t[:, 1], t[:, 0], t[:, 1], ALU.mult).then_inc(s_glu, 1)
                pool.wait_ge(s_wbc, u + 1)
                pool.wait_ge(s_glu, u + 1)
                nc.gpsimd.tensor_tensor(t[:, 1], t[:, 1], t[:, 2], ALU.mult).then_inc(s_glw, 1)

            for i in range(-1, 19):
                for c in {7: (1,), 8: (3,), 11: (7,), 14: (9,)}.get(i, ()):
                    expert(0, c)
                for c in {6: (3,)}.get(i, ()):
                    w_lo(P_GU + 2 + c)
                if 0 <= i < NG - 1:
                    k_lo(i + 1)
                for c in {18: (11,)}.get(i, ()):
                    expert(0, c)
                for c in {5: (1,)}.get(i, ()):
                    w_lo(P_GU + 2 + c)
                if 3 <= i < NG + 3:
                    gap_exp(i - 3)
                for c in {4: (0,), 5: (2,), 7: (4,)}.get(i, ()):
                    w_lo(P_GU + 2 + c)
                for c in {8: (4, 5), 10: (6,), 11: (8,), 14: (10,)}.get(i, ()):
                    expert(0, c)
                if i < NG - 2:
                    k_norm(i + 2)
                if 0 <= i < NG:
                    probs(i)
                if 2 <= i < NG + 2:
                    root(i - 2, SIZES[i - 2], s_ve, s_rstd)
                for c in {6: (0,), 7: (2,)}.get(i, ()):
                    expert(0, c)
                for c in {7: (5,)}.get(i, ()):
                    w_lo(P_GU + 2 + c)
            w_lo(P_DN)
            for c in range(NT):
                expert(1, c)
                if c % 3 == 1 and c < 9:
                    w_lo(P_DN + 1 + c // 3)
            for j in range(ND):
                root(j, TD, s_zve, s_zrstd)

        @block.scalar
        def _(act):
            def w_hi(k):
                _, n, place, dst = pieces[k]
                act.wait_ge(*arrival(k))
                if k >= P_DN:
                    act.wait_ge(s_op, NG)
                elif k >= P_GU + 2:
                    act.wait_ge(s_v, NG)
                nc.scalar.activation(dst[:, 0, :], place, ACT.Copy).then_inc(s_xhi if k < NC else s_whi, 1)
            w_hi(0)
            act.wait_ge(s_small, 16)
            nc.scalar.activation(small_hi[:, :], sm[:, C_WR:C_SMALL], ACT.Copy).then_inc(s_smhi, 1)
            for c in range(1, NC):
                w_hi(c)
            w_hi(P_QKV)
            w_hi(P_QKV + 1)
            for t in range(2):
                act.wait_ge(s_tok, 2 * NC - 1 + t)
                nc.scalar.activation(two(hT[:, t]), halves(4 + 2 * t), ACT.Identity,
                                     bias=sm[:, C_TOKB + t:C_TOKB + t + 1]).then_inc(s_hthi, 1)

            def root(t):
                act.wait_ge(s_nsum, t + 1)
                nc.scalar.activation(two(rnorm[:, t]), halves(slot["sum", t]), ACT.Sqrt).then_inc(s_nsqrt, 1)

            def ss_hi(t):
                act.wait_ge(s_ssk if t else s_ssq, 5)
                nc.scalar.activation(ss_r[:, t, 0], ss[:, t], ACT.Copy).then_inc(s_sshi, 1)

            act.wait_ge(s_const, 1)
            w_next = P_QKV + 2
            for m in range(12):
                if m == 7:
                    ss_hi(0)
                act.wait_ge(s_qk, m + 1)
                if m % 6 >= 3:
                    act.wait_ge(s_ssk if m >= 6 else s_ssq, m % 6 - 2)
                dst = ss[:, m // 6] if m % 6 == 0 else sq[:, m % 2]
                if m in (7, 8):
                    act.wait_ge(s_ssq, 5)
                nc.scalar.activation(two(dst), halves(slot["qk", m]), ACT.Square).then_inc(s_sq, 1)
                if w_next < P_GU + 2 and m != 6:
                    w_hi(w_next)
                    w_next += 1
            root(0)

            def v_hi(g):
                n = SIZES[g]
                act.wait_ge(s_v, g + 1)
                nc.scalar.activation(V[0:n, g, 0].rearrange("p (a n) -> p a n", a=2),
                                     ps[0:n, slot["v", g]:slot["v", g] + 2, 0:PD // 2], ACT.Copy).then_inc(s_vhi, 1)
            def norm_ln(t):
                act.wait_ge(s_nsqrt, t + 1)
                nc.scalar.activation(rnorm[:, t, GRP:T], rnorm[:, t, GRP:T], ACT.Ln, bias=small_eps[:, :]).then_inc(s_nln, 1)

            def norm_exp(t):
                act.wait_ge(s_nln, t + 1)
                nc.scalar.activation(rnorm[:, t, GRP:T], rnorm[:, t, GRP:T], ACT.Exp, scale=-0.5).then_inc(s_r, 1)

            def k_hi(g):
                n, o = SIZES[g], OFFS[g]
                if g == 0:
                    act.wait_ge(s_kn0, 1)
                else:
                    act.wait_ge(s_kn, g)
                    act.wait_ge(s_s, g)
                for a in range(2):
                    r = slice(64 * a, 64 * a + 64)
                    nc.scalar.activation(K[r, 0, :, a, 0:n], qk_raw[r, NP:2 * NP, o:o + n], ACT.Copy).then_inc(s_khi, 1)

            def q_hi(g):
                n, o = SIZES[g], OFFS[g]
                act.wait_ge(s_qn, g + 1)
                if g >= 1:
                    act.wait_ge(s_s, g)
                nc.scalar.activation(Q[:, 0, :, 0:n], qk_raw[:, 0:NP, o:o + n], ACT.Copy).then_inc(s_qhi, 1)

            def o_hi(g):
                n = SIZES[g]
                act.wait_ge(s_pv, g + 1)
                if g >= 1:
                    act.wait_ge(s_op, g)
                for a in range(2):
                    nc.scalar.activation(oT[64 * a:64 * a + 64, 0, :, 0:n].rearrange("p (b m) n -> p b m n", b=NB),
                                         ps[64 * a:64 * a + 64, 3:6, 0:HB * n].rearrange(
                                             "p b (m a n) -> p b m a n", m=2, a=2)[:, :, :, a], ACT.Copy)\
                        .then_inc(s_ohi, 1)

            def pt_hi(g):
                n = SIZES[g]
                act.wait_ge(s_pt, g + 1)
                if g >= 1:
                    act.wait_ge(s_pv, g)
                for b in range(NB):
                    nc.scalar.activation(PT[0:n, 0, b * HB * n:(b + 1) * HB * n], ps[0:n, 3 + b, 0:HB * n],
                                         ACT.Copy).then_inc(s_pthi, 1)

            def h1_hi(g):
                n, o = SIZES[g], OFFS[g]
                act.wait_ge(s_ht1, g + 1)
                nc.scalar.activation(h1T[:, 0:2, o:o + n], ps[:, 7, 0:2 * n].rearrange("p (k n) -> p k n", k=2),
                                     ACT.Copy).then_inc(s_h1hi, 1)

            def exps(g):
                n = SIZES[g]
                act.wait_ge(s_sub, g + 1)
                if g >= 1:
                    if g >= 2:
                        act.wait_ge(s_pt, g - 1)
                    act.wait_ge(s_rinv, g)
                for h in range(H):
                    nc.scalar.activation(Pr[0:n, g % 2, h * n:(h + 1) * n], ps[0:n, h // HB, (h % HB) * n:(h % HB + 1) * n],
                                         ACT.Exp, accum_out=psum_e[0:n, h:h + 1])\
                        .then_inc(s_e, 1)

            def w_hi_t(g):
                n, o = SIZES[g], OFFS[g]
                act.wait_ge(s_wt, g + 1)
                nc.scalar.activation(w2T[:, o:o + n], ps[0:40, 7, 256:256 + n], ACT.Copy).then_inc(s_wthi, 1)

            def expert(a, c):
                u = NT * a + c
                t = tmp[:, u % 4]
                act.wait_ge(s_g, u + 1)
                if u >= 4:
                    act.wait_ge(s_act, u - 3)
                nc.scalar.activation(t[:, 1], t[:, 0], ACT.Sigmoid, scale=ALPHA).then_inc(s_sig, 1)
                act.wait_ge(s_gu, 3 * u + 3)
                nc.scalar.activation(t[:, 2], ps[:, gu_bank(a, c, 2), 0:TH], ACT.Copy).then_inc(s_wbc, 1)
                if u >= 1:
                    act_hi(u - 1)

            def act_hi(u):
                act.wait_ge(s_act, u + 1)
                if u == NT:
                    act.wait_ge(s_pv, NG)
                nc.scalar.activation(acts[:, u // NT, u % NT, 0], tmp[:, u % 4, 4], ACT.Copy).then_inc(s_ahi, 1)

            def first_root(t):
                act.wait_ge(s_rec0, t + 1)
                nc.scalar.activation(rnorm[:, t, 0:GRP], rnorm[:, t, 0:GRP], ACT.Sqrt).then_inc(s_r0, 1)

            ss_hi(1)
            first_root(0)
            v_hi(0)
            v_hi(1)
            root(1)
            q_hi(0)
            first_root(1)
            v_hi(2)
            k_hi(0)
            v_hi(3)
            norm_ln(0)
            norm_ln(1)
            norm_exp(0)
            norm_exp(1)
            v_hi(4)
            v_hi(5)
            for i in range(0, 18):
                for c in {9: (3,), 13: (8,), 14: (10,)}.get(i, ()):
                    expert(0, c)
                for c in {4: (1,)}.get(i, ()):
                    w_hi(P_GU + 2 + c)
                if 1 <= i < NG + 1:
                    exps(i - 1)
                for c in {7: (0,)}.get(i, ()):
                    expert(0, c)
                if 2 <= i < NG + 2:
                    o_hi(i - 2)
                for c in {8: (2,), 10: (5, 6), 17: (11,)}.get(i, ()):
                    expert(0, c)
                for c in {3: (0,), 5: (2, 3), 6: (4,), 8: (5,)}.get(i, ()):
                    w_hi(P_GU + 2 + c)
                if i < NG - 1:
                    k_hi(i + 1)
                if i < NG - 1:
                    q_hi(i + 1)
                for c in {9: (4,), 13: (9,)}.get(i, ()):
                    expert(0, c)
                if 4 <= i < NG + 4:
                    w_hi_t(i - 4)
                for c in {11: (7,)}.get(i, ()):
                    expert(0, c)
                if 1 <= i < NG + 1:
                    pt_hi(i - 1)
                if 3 <= i < NG + 3:
                    h1_hi(i - 3)
                for c in {7: (1,)}.get(i, ()):
                    expert(0, c)
            w_hi(P_DN)
            for c in range(NT):
                expert(1, c)
                if c % 3 == 0 and c < 9:
                    w_hi(P_DN + 1 + c // 3)
            act_hi(2 * NT - 1)

        @block.vector
        def _(dve):
            def x_lo(c):
                _, n, place, dst = pieces[c]
                dve.wait_ge(*arrival(c))
                dve.wait_ge(s_xhi if c < NC else s_whi, c + 1 if c < NC else 1)
                nc.vector.tensor_tensor(dst[:, 1, :], place, f(dst[:, 0, :]), ALU.subtract)\
                    .then_inc(s_xlo if c < NC else s_w6lo, 1)
            x_lo(0)
            dve.wait_ge(s_small, 16)
            nc.vector.reciprocal(inv_scale[:, :], sm[:, C_SCALE:C_SCALE + NP]).then_inc(s_smprep, 1)
            nc.vector.tensor_scalar_add(bup1[:, :], sm[:, C_BGU:C_BGU + 2 * NT].rearrange(
                "p (s u k) -> p s u k", s=NPAIR, u=2)[:, :, 1], 1.0).then_inc(s_smprep, 1)
            dve.wait_ge(s_smhi, 1)
            nc.vector.tensor_tensor(small_lo[:, :], sm[:, C_WR:C_SMALL], f(small_hi[:, :]),
                                    ALU.subtract).then_inc(s_smlo, 1)
            nc.vector.memset(small_eps[:, :], NORM_EPS)
            nc.vector.memset(w2[:, :], 0.0)
            for c in range(1, NC + 1):
                x_lo(c)
            dve.wait_ge(s_hthi, 1)
            nc.vector.scalar_tensor_tensor(out=two(hT[:, 2]), in0=halves(4), scalar=sm[:, C_TOKB:C_TOKB + 1],
                                           in1=two(f(hT[:, 0])), op0=ALU.add, op1=ALU.subtract).then_inc(s_htlo, 1)
            dve.wait_ge(s_hthi, 2)
            up = slice(64, 128)
            nc.vector.scalar_tensor_tensor(out=two(hT[up, 1]), in0=ps[up, 6:8, 0:TH],
                                           scalar=sm[up, C_TOKB + 1:C_TOKB + 2], in1=two(f(hT[up, 1])),
                                           op0=ALU.add, op1=ALU.subtract).then_inc(s_htlo, 1)
            dve.wait_ge(s_sel, 7)
            nc.vector.tensor_copy(ident_r[:, :], ident[:, :])
            nc.vector.tensor_scalar(minus_r[:, :], ident[:, :], -1.0, None, ALU.mult)
            nc.vector.tensor_copy(fold_r[:, :], fold_f)
            nc.vector.tensor_copy(onehot[:, :, :], onehot_f)
            nc.vector.tensor_copy(mask_l[:, :], mask_lf)
            nc.vector.tensor_copy(mask_r[:, :], mask_rf).then_inc(s_const, 1)

            def ss_lo(t):
                dve.wait_ge(s_sshi, t + 1)
                nc.vector.tensor_tensor(ss_r[:, t, 1], ss[:, t], f(ss_r[:, t, 0]), ALU.subtract).then_inc(s_sslo, 1)

            dve.wait_ge(s_smprep, 1)
            for m in range(12):
                dve.wait_ge(s_sq, m + 1)
                if m < NP:
                    nc.vector.tensor_scalar(two(qk_raw[:, m]), halves(slot["qk", m]), inv_scale[:, m:m + 1], None,
                                            ALU.mult).then_inc(s_raw, 1)
                else:
                    nc.vector.tensor_copy(two(qk_raw[:, m]), halves(slot["qk", m])).then_inc(s_raw, 1)
                if 1 <= m < NP:
                    if m > 1:
                        dve.wait_ge(s_ssq, m - 1)
                    nc.vector.tensor_tensor(ss[:, 0], ss[:, 0], sq[:, m % 2], ALU.add).then_inc(s_ssq, 1)
                if m == 7:
                    ss_lo(0)
            ss_lo(1)

            def v_lo(g):
                n = SIZES[g]
                dve.wait_ge(s_vhi, g + 1)
                nc.vector.tensor_tensor(V[0:n, g, 1].rearrange("p (a n) -> p a n", a=2),
                                        ps[0:n, slot["v", g]:slot["v", g] + 2, 0:PD // 2],
                                        f(V[0:n, g, 0]).rearrange("p (a n) -> p a n", a=2),
                                        ALU.subtract).then_inc(s_vlo, 1)

            def q_norm(g):
                n, o = SIZES[g], OFFS[g]
                qq = qk_raw[:, 0:NP, o:o + n]
                if g == 0:
                    dve.wait_ge(s_r0, 1)
                    dve.wait_ge(s_raw, NP)
                elif g == 1:
                    dve.wait_ge(s_r, 1)
                nc.vector.tensor_tensor(qq, qq, rnorm[:, 0:1, o:o + n].to_broadcast([128, NP, n]),
                                        ALU.mult).then_inc(s_qn, 1)

            def q_split(g):
                n, o = SIZES[g], OFFS[g]
                qq = qk_raw[:, 0:NP, o:o + n]
                dve.wait_ge(s_qhi, g + 1)
                nc.vector.tensor_tensor(Q[:, 1, :, 0:n], qq, f(Q[:, 0, :, 0:n]),
                                        ALU.subtract).then_inc(s_qlo, 1)

            def row_max(g):
                n = SIZES[g]
                dve.wait_ge(s_s, g + 1)
                nc.vector.reduce_max(mx_r[0:n, :], ps[0:n, 0:NB, 0:HB * n].rearrange("p b (h j) -> p b h j", h=HB),
                                     X).then_inc(s_mx, 1)

            def sum_recip(g):
                n = SIZES[g]
                dve.wait_ge(s_e, H * (g + 1))
                if g >= 1:
                    dve.wait_ge(s_p, g)
                nc.vector.reciprocal(rinv[0:n, :], psum_e[0:n, :]).then_inc(s_rinv, 1)

            def o_lo(g):
                n = SIZES[g]
                for a in range(2):
                    dve.wait_ge(s_ohi, 2 * (g + 1))
                    r = slice(64 * a, 64 * a + 64)
                    nc.vector.tensor_tensor(oT[r, 1, :, 0:n].rearrange("p (b m) n -> p b m n", b=NB),
                                            ps[r, 3:6, 0:HB * n].rearrange("p b (m a n) -> p b m a n", m=2, a=2)[:, :, :, a],
                                            f(oT[r, 0, :, 0:n]).rearrange("p (b m) n -> p b m n", b=NB),
                                            ALU.subtract).then_inc(s_olo, 1)

            def pt_lo(g):
                n = SIZES[g]
                for b in range(NB):
                    dve.wait_ge(s_pthi, NB * g + b + 1)
                    cols = slice(b * HB * n, (b + 1) * HB * n)
                    nc.vector.tensor_tensor(PT[0:n, 1, cols], ps[0:n, 3 + b, 0:HB * n], f(PT[0:n, 0, cols]),
                                            ALU.subtract).then_inc(s_ptlo, 1)

            def h1_lo(g):
                n, o = SIZES[g], OFFS[g]
                dve.wait_ge(s_h1hi, g + 1)
                nc.vector.tensor_tensor(h1T[:, 2, o:o + n], ps[:, 7, 0:n], f(h1T[:, 0, o:o + n]),
                                        ALU.subtract).then_inc(s_h1lo, 1)
                nc.vector.tensor_tensor(h1T[up, 1, o:o + n], ps[up, 7, n:2 * n], f(h1T[up, 1, o:o + n]),
                                        ALU.subtract).then_inc(s_h1lo, 1)

            def w_lo_t(g):
                n, o = SIZES[g], OFFS[g]
                dve.wait_ge(s_wthi, g + 1)
                nc.vector.tensor_tensor(w2T[32:40, o:o + n], ps[32:40, 7, 256:256 + n], f(w2T[32:40, o:o + n]),
                                        ALU.subtract).then_inc(s_wtlo, 1)

            def statistics(g, src, st_done, mv_done, ve_done):
                n = src.shape[0]
                nc.vector.bn_stats(stats[0:n, :], src).then_inc(st_done, 1)
                dve.wait_ge(st_done, g + 1)
                nc.vector.bn_aggr(mv[0:n, :], stats[0:n, :]).then_inc(mv_done, 1)
                dve.wait_ge(mv_done, g + 1)
                nc.vector.tensor_scalar_add(var_e[0:n, :], mv[0:n, 1:2], LN_EPS).then_inc(ve_done, 1)

            def ln1_stats(g):
                n = SIZES[g]
                dve.wait_ge(s_op, g + 1)
                if g >= 1:
                    dve.wait_ge(s_h1, 2 * g)
                statistics(g, ps[0:n, 6, 0:D], s_st, s_mv, s_ve)

            def ln1(g):
                n = SIZES[g]
                dve.wait_ge(s_rstd, g + 1)
                if g >= 2:
                    dve.wait_ge(s_ht1, g - 1)
                for dst, src in ((slice(0, D), slice(0, D)), (slice(D, 256), slice(DA, D))):
                    nc.vector.tensor_scalar(h1[0:n, g % 2, dst], ps[0:n, 6, src], mv[0:n, 0:1], rstd[0:n, 0:1],
                                            ALU.subtract, ALU.mult).then_inc(s_h1, 1)

            def router_top(g):
                n = SIZES[g]
                dve.wait_ge(s_rt, g + 1)
                nc.vector.tensor_tensor(lg[0:n, :], ps[0:n, 7, 384:392], sm[0:n, C_BR:C_BR + 8],
                                        ALU.add).then_inc(s_lg, 1)
                dve.wait_ge(s_lg, g + 1)
                nc.vector.max(top[0:n, :], lg[0:n, :]).then_inc(s_top, 1)
                dve.wait_ge(s_top, g + 1)
                nc.vector.tensor_tensor(rt[0:n, 2:3], top[0:n, 1:2], top[0:n, 0:1], ALU.subtract).then_inc(s_gap, 1)
                nc.vector.max_index(top_i[0:n, :], top[0:n, :], lg[0:n, :]).then_inc(s_ti, 1)
                dve.wait_ge(s_ti, 3 * g + 1)
                nc.vector.tensor_copy(rt[0:n, 0:2], top_i[0:n, 0:2]).then_inc(s_ti, 1)

            def router_weights(g):
                n = SIZES[g]
                dve.wait_ge(s_egap, g + 1)
                nc.vector.tensor_scalar_add(rt[0:n, 6:7], rt[0:n, 3:4], 1.0).then_inc(s_rs, 1)
                dve.wait_ge(s_rs, g + 1)
                nc.vector.reciprocal(rt[0:n, 4:5], rt[0:n, 6:7]).then_inc(s_p1, 1)
                dve.wait_ge(s_p1, g + 1)
                nc.vector.tensor_tensor(rt[0:n, 5:6], rt[0:n, 3:4], rt[0:n, 4:5], ALU.mult).then_inc(s_p2, 1)
                dve.wait_ge(s_ti, 3 * g + 2)
                iota = sm[0:n, C_IOTA:C_IOTA + 8]
                nc.vector.tensor_scalar(sel[0:n, 0], iota, rt[0:n, 0:1], rt[0:n, 4:5], ALU.is_equal,
                                        ALU.mult).then_inc(s_ti, 1)
                dve.wait_ge(s_p2, g + 1)
                nc.vector.tensor_scalar(sel[0:n, 1], iota, rt[0:n, 1:2], rt[0:n, 5:6], ALU.is_equal,
                                        ALU.mult).then_inc(s_sel2, 1)
                dve.wait_ge(s_sel2, g + 1)
                if g >= 1:
                    dve.wait_ge(s_wt, g)
                nc.vector.tensor_tensor(w2[0:n, 0:8], sel[0:n, 0], sel[0:n, 1], ALU.add).then_inc(s_w2, 1)
                nc.vector.tensor_tensor(w2[0:n, 32:40], sel[0:n, 0], sel[0:n, 1], ALU.add).then_inc(s_w2, 1)

            def expert_in(a, c):
                u = NT * a + c
                s, k = divmod(c, 3)
                t = tmp[:, u % 4]
                cg = C_BGU + 6 * s + k
                dve.wait_ge(s_gu, 3 * u + 1)
                if u >= 4:
                    dve.wait_ge(s_alo, u - 3)
                nc.vector.tensor_scalar(t[:, 0], ps[:, gu_bank(a, c, 0), 0:TH], sm[:, cg:cg + 1], LIMIT,
                                        ALU.add, ALU.min).then_inc(s_g, 1)
                dve.wait_ge(s_gu, 3 * u + 2)
                nc.vector.tensor_scalar(t[:, 3], ps[:, gu_bank(a, c, 1), 0:TH], bup1[:, c:c + 1], LIMIT + 1,
                                        ALU.add, ALU.min).then_inc(s_u, 1)
                if u >= 1:
                    expert_act(u - 1)
                if u >= 2:
                    expert_lo(u - 2)

            def expert_act(u):
                t = tmp[:, u % 4]
                dve.wait_ge(s_glw, u + 1)
                dve.wait_ge(s_u, u + 1)
                nc.vector.scalar_tensor_tensor(out=t[:, 4], in0=t[:, 3], scalar=1.0 - LIMIT, in1=t[:, 1],
                                               op0=ALU.max, op1=ALU.mult).then_inc(s_act, 1)

            def expert_lo(u):
                dve.wait_ge(s_ahi, u + 1)
                a, c = divmod(u, NT)
                nc.vector.tensor_tensor(acts[:, a, c, 1], tmp[:, u % 4, 4], f(acts[:, a, c, 0]),
                                        ALU.subtract).then_inc(s_alo, 1)

            def ln2(j):
                tile = ps[0:TD, down_bank(j), 0:D]
                dve.wait_ge(s_dn, j + 1)
                statistics(j, tile, s_zst, s_zmv, s_zve)
                dve.wait_ge(s_zrstd, j + 1)
                if j >= 2:
                    dve.wait_ge(s_out[j % 2], 16 * (j // 2))
                nc.vector.tensor_scalar(res[0:TD, j % 2, :], tile, mv[0:TD, 0:1], rstd[0:TD, 0:1],
                                        ALU.subtract, ALU.mult).then_inc(s_res, 1)

            def first_norm(t):
                dve.wait_ge(s_nsqrt, t + 1)
                nc.vector.tensor_scalar_add(rnorm[:, t, 0:GRP], rnorm[:, t, 0:GRP], NORM_EPS).then_inc(s_eps0, 1)
                dve.wait_ge(s_eps0, t + 1)
                nc.vector.reciprocal(rnorm[:, t, 0:GRP], rnorm[:, t, 0:GRP]).then_inc(s_rec0, 1)

            def first_k():
                kk = qk_raw[:, NP:2 * NP, 0:GRP]
                dve.wait_ge(s_r0, 2)
                dve.wait_ge(s_raw, 12)
                nc.vector.tensor_tensor(kk, kk, rnorm[:, 1:2, 0:GRP].to_broadcast([128, NP, GRP]),
                                        ALU.mult).then_inc(s_kn0, 1)

            def first_k_lo():
                for a in range(2):
                    dve.wait_ge(s_khi, a + 1)
                    r = slice(64 * a, 64 * a + 64)
                    nc.vector.tensor_tensor(K[r, 1, :, a, 0:GRP], qk_raw[r, NP:2 * NP, 0:GRP], f(K[r, 0, :, a, 0:GRP]),
                                            ALU.subtract).then_inc(s_klo0, 1)

            first_norm(0)
            q_norm(0)
            v_lo(0)
            v_lo(1)
            first_norm(1)
            first_k()
            v_lo(2)
            q_split(0)
            first_k_lo()
            for g in range(3, NG):
                v_lo(g)
            for i in range(-2, 14):
                for c in {12: (7, 8)}.get(i, ()):
                    expert_in(0, c)
                if 0 <= i < NG:
                    row_max(i)
                for c in {12: (9, 10)}.get(i, ()):
                    expert_in(0, c)
                if 3 <= i < NG + 3:
                    ln1(i - 3)
                for c in {9: (5,)}.get(i, ()):
                    expert_in(0, c)
                if 4 <= i < NG + 4:
                    w_lo_t(i - 4)
                for c in {7: (1,)}.get(i, ()):
                    expert_in(0, c)
                if 1 <= i < NG + 1:
                    pt_lo(i - 1)
                for c in {8: (3,)}.get(i, ()):
                    expert_in(0, c)
                if 3 <= i < NG + 3:
                    h1_lo(i - 3)
                for c in {13: (11,)}.get(i, ()):
                    expert_in(0, c)
                if 3 <= i < NG + 3:
                    router_top(i - 3)
                if 0 <= i < NG - 1:
                    q_split(i + 1)
                for c in {6: (0,), 8: (4,)}.get(i, ()):
                    expert_in(0, c)
                if i < NG - 3:
                    q_norm(i + 3)
                if 2 <= i < NG + 2:
                    ln1_stats(i - 2)
                for c in {7: (2,)}.get(i, ()):
                    expert_in(0, c)
                if 3 <= i < NG + 3:
                    router_weights(i - 3)
                if 0 <= i < NG:
                    sum_recip(i)
                for c in {9: (6,)}.get(i, ()):
                    expert_in(0, c)
                if 1 <= i < NG + 1:
                    o_lo(i - 1)
            for c in range(NT):
                expert_in(1, c)
            expert_act(2 * NT - 1)
            expert_lo(2 * NT - 2)
            expert_lo(2 * NT - 1)
            for j in range(ND):
                ln2(j)

        @block.tensor
        def _(pe):
            mm = nc.tensor.matmul

            def keep_warm(n):
                for _ in range(n):
                    mm(ps[:, 3, :], filler[:, 0:128], filler[:, :], start=True, stop=True)

            pe.wait_ge(s_filler, 1)
            keep_warm(14)
            for c in range(NC):
                pe.wait_ge(s_xlo, c + 1)
                hi, lo = xw[:, c, 0], xw[:, c, 1]
                for t in range(2):
                    for wx, px in ((hi, hi), (hi, lo), (lo, hi)):
                        for a in range(2):
                            last = mm(ps[:, 4 + 2 * t + a, 0:TH], wx[:, T + 128 * t:T + 128 * t + 128],
                                      px[:, TH * a:TH * a + TH], start=(c == 0 and wx is hi and px is hi),
                                      stop=(c == NC - 1 and wx is lo))
                    last.then_inc(s_tok, 1)

            def wide(bank, w_a, w_b, x, a, first=False):
                cols = slice(TH * a, TH * a + TH)
                out_ap = ps[:, bank, 0:TH]
                mm(out_ap, w_a(0), x[:, 0, cols], start=True, stop=False)
                mm(out_ap, w_a(1), x[:, 0, cols], start=False, stop=False)
                if first:
                    pe.wait_ge(s_htlo, 1)
                mm(out_ap, w_a(0), x[:, 2, cols], start=False, stop=False)
                if first:
                    pe.wait_ge(s_htlo, 2)
                mm(out_ap, w_b(0), x[:, 1, cols], start=False, stop=False)
                return mm(out_ap, w_b(1), x[:, 1, cols], start=False, stop=True)

            def norm_sum(t):
                pe.wait_ge(s_const, 1)
                pe.wait_ge(s_sslo, t + 1)
                pe.wait_ge(*slot_read(("sum", t)))
                for a in range(2):
                    for k in range(2):
                        last = mm(ps[:, slot["sum", t] + a, 0:TH], fold_r[:, :], ss_r[:, t, k, TH * a:TH * a + TH],
                                  start=(k == 0), stop=(k == 1))
                last.then_inc(s_nsum, 1)

            keep_warm(6)
            pe.wait_ge(s_hthi, 1)
            for m in range(12):
                s, p = divmod(m, NP)
                if m == 0:
                    pe.wait_ge(s_w6lo, 1)
                pe.wait_ge(s_wlo, w_ready(P_QKV + 2 * s + 1))
                if slot_read(("qk", m)):
                    pe.wait_ge(*slot_read(("qk", m)))
                cols = slice(128 * p, 128 * p + 128)
                for a in range(2):
                    last = wide(slot["qk", m] + a, lambda k: wqkv[:, s, 0, k, cols],
                                lambda k: wqkv[:, s, 1, k, cols], hT, a, m == 0 and a == 0)
                last.then_inc(s_qk, 1)
                if m == 10:
                    norm_sum(0)

            def v_proj(g):
                n, o = SIZES[g], OFFS[g]
                if g == 0:
                    pe.wait_ge(s_wlo, w_ready(P_QKV + 5))
                pe.wait_ge(*slot_read(("v", g)))
                tok = slice(o, o + n)
                for a in range(2):
                    cols = slice(PD // 2 * a, PD // 2 * (a + 1))
                    out_ap = ps[0:n, slot["v", g] + a, 0:PD // 2]
                    mm(out_ap, hT[:, 0, tok], wqkv[:, 2, 0, 0, cols], start=True, stop=False)
                    mm(out_ap, hT[:, 0, tok], wqkv[:, 2, 0, 1, cols], start=False, stop=False)
                    mm(out_ap, hT[:, 2, tok], wqkv[:, 2, 0, 0, cols], start=False, stop=False)
                    mm(out_ap, hT[:, 1, tok], wqkv[:, 2, 1, 0, cols], start=False, stop=False)
                    last = mm(out_ap, hT[:, 1, tok], wqkv[:, 2, 1, 1, cols], start=False, stop=True)
                last.then_inc(s_v, 1)

            for g in range(3):
                v_proj(g)
            norm_sum(1)
            v_proj(3)

            def scores(g):
                n = SIZES[g]
                pe.wait_ge(s_qlo, g + 1)
                if g == 0:
                    pe.wait_ge(s_klo0, 2)
                    pe.wait_ge(s_nsqrt, 2)
                else:
                    pe.wait_ge(s_klo, 2 * g)
                for b in range(NB):
                    if g == 0 and b == 2:
                        pe.wait_ge(s_vlo, 4)
                    if g >= 1:
                        pe.wait_ge(s_e, H * (g - 1) + HB * (b + 1))
                    mm(ps[0:n, b, 0:HB * n], mask_l[:, 0:n],
                       mask_r[:, :].rearrange("p (h j) -> p h j", h=HB)[:, :, 0:n], start=True, stop=False,
                       skip_group_check=True)
                    for j in range(2):
                        m = 2 * b + j
                        for qp, kp in ((0, 0), (0, 1), (1, 0)):
                            last = mm(ps[0:n, b, 2 * n * j:2 * n * (j + 1)], Q[:, qp, m, 0:n], K[:, kp, m, :, 0:n],
                                      start=False, stop=False, skip_group_check=True)
                last.then_inc(s_s, 1)

            def subtract_max(g):
                n = SIZES[g]
                pe.wait_ge(s_mx, g + 1)
                for b in range(NB):
                    last = mm(ps[0:n, b, 0:HB * n], minus_r[0:n, 0:n],
                              mx_r[0:n, HB * b:HB * b + HB].unsqueeze(2).to_broadcast([n, HB, n]),
                              start=False, stop=True, skip_group_check=True)
                last.then_inc(s_sub, 1)

            def p_transpose(g):
                n = SIZES[g]
                if g == 0:
                    pe.wait_ge(s_vlo, NG)
                if g >= 1:
                    pe.wait_ge(s_olo, 2 * g)
                keep_warm(3)
                pe.wait_ge(s_p, g + 1)
                for h in range(H):
                    last = nc.tensor.transpose(ps[0:n, 3 + h // HB, (h % HB) * n:(h % HB + 1) * n],
                                               Pr[0:n, g % 2, h * n:(h + 1) * n], ident[0:n, 0:n])
                last.then_inc(s_pt, 1)

            def weighted(g):
                n = SIZES[g]
                for p in range(NP):
                    b = p // 2
                    pe.wait_ge(s_ptlo, NB * g + b + 1)
                    pe.wait_ge(s_vlo, g + 1)
                    out_ap = ps[:, 3 + b, (p % 2) * 2 * n:(p % 2 + 1) * 2 * n]
                    for vp, pp in ((0, 0), (0, 1), (1, 0)):
                        last = mm(out_ap, V[0:n, g, vp, 128 * p:128 * p + 128], PT[0:n, pp, 2 * p * n:2 * (p + 1) * n],
                                  start=(vp == 0 and pp == 0), stop=(vp == 1))
                last.then_inc(s_pv, 1)

            def project(g):
                n, o = SIZES[g], OFFS[g]
                pe.wait_ge(s_olo, 2 * (g + 1))
                pe.wait_ge(s_wlo, w_ready(P_OUT + 1))
                if g >= 1:
                    pe.wait_ge(s_h1, 2 * g)
                tok = slice(o, o + n)
                for p in range(NP):
                    for op_, wp in ((0, 0), (0, 1), (1, 0)):
                        mm(ps[0:n, 6, 0:D], oT[:, op_, p, 0:n], wout[:, p // 3, wp, p % 3, :],
                           start=(p == 0 and op_ == 0 and wp == 0), stop=False)
                pick = ident_r[:, BOUT_ROW:BOUT_ROW + 1].to_broadcast([128, n])
                mm(ps[0:n, 6, 0:D], pick, small_hi[:, 16:16 + D], start=False, stop=False)
                mm(ps[0:n, 6, 0:D], pick, small_lo[:, 16:16 + D], start=False, stop=False)
                residual(ps[0:n, 6], hT, tok, True).then_inc(s_op, 1)

            def residual(bank, x, tok, stop):
                mm(bank[:, 0:DA], x[:, 0, tok], ident_r[:, :], start=False, stop=False)
                mm(bank[:, 0:DA], x[:, 2, tok], ident_r[:, :], start=False, stop=False)
                return mm(bank[:, DA:D], x[:, 1, tok], fold_r[:, 0:DB], start=False, stop=stop)

            def h1_transpose(g):
                n = SIZES[g]
                pe.wait_ge(s_h1, 2 * (g + 1))
                if g >= 1:
                    pe.wait_ge(s_wtlo, g)
                for k in range(2):
                    last = nc.tensor.transpose(ps[:, 7, k * n:(k + 1) * n], h1[0:n, g % 2, 128 * k:128 * k + 128],
                                               ident[0:n, 0:n])
                last.then_inc(s_ht1, 1)

            def logits(g):
                n, o = SIZES[g], OFFS[g]
                tok = slice(o, o + n)
                pe.wait_ge(s_h1lo, 2 * (g + 1))
                out_ap = ps[0:n, 7, 384:392]
                a_hi, a_lo, b_hi, b_lo = small_hi[:, 0:8], small_lo[:, 0:8], small_hi[:, 8:16], small_lo[:, 8:16]
                mm(out_ap, h1T[:, 0, tok], a_hi, start=True, stop=False)
                mm(out_ap, h1T[:, 0, tok], a_lo, start=False, stop=False)
                mm(out_ap, h1T[:, 2, tok], a_hi, start=False, stop=False)
                mm(out_ap, h1T[:, 1, tok], b_hi, start=False, stop=False)
                mm(out_ap, h1T[:, 1, tok], b_lo, start=False, stop=True).then_inc(s_rt, 1)

            def w_transpose(g):
                n = SIZES[g]
                pe.wait_ge(s_w2, 2 * (g + 1))
                nc.tensor.transpose(ps[0:40, 7, 256:256 + n], w2[0:n, :], ident[0:n, 0:n]).then_inc(s_wt, 1)

            def expert(a, c):
                n = NT * a + c
                s, k = divmod(c, 3)
                if n == 0:
                    pe.wait_ge(s_e, H * NG)
                if c == 0:
                    pe.wait_ge(s_wtlo, 3 if a == 0 else NG)
                if a == 0:
                    pe.wait_ge(s_wlo, w_ready(P_GU + 2 * GU_ORDER.index(s) + 1))
                for u in range(3):
                    back = 2 if u < 2 and n >= NT + 2 else 1
                    if n == NT + 1 and u < 2:
                        pe.wait_ge(s_h1, 2 * NG)
                    elif n >= back:
                        pe.wait_ge((s_g, s_u, s_wbc)[u], n - back + 1)
                    bank = gu_bank(a, c, u)
                    if u < 2:
                        cols = slice(384 * u + 128 * k, 384 * u + 128 * k + 128)
                        last = wide(bank, lambda j: wgu[:, s, 0, j, cols], lambda j: wgu[:, s, 1, j, cols], h1T, a)
                    else:
                        first = 256 * s + (0, 128, 64)[k]
                        w = onehot[:, :, :].rearrange("p e n -> p (e n)")[:, first:first + 128]
                        last = mm(ps[:, bank, 0:TH], w, w2T[:, TH * a:TH * a + TH], start=True, stop=True)
                    last.then_inc(s_gu, 1)

            def down_bias(j):
                tok = slice(TD * j, TD * j + TD)
                bank = ps[0:TD, down_bank(j)]
                mm(bank[:, 0:D], w2T[:, tok], small_hi[0:40, 16:16 + D], start=True, stop=False)
                mm(bank[:, 0:D], w2T[:, tok], small_lo[0:40, 16:16 + D], start=False, stop=False)
                residual(bank, h1T, tok, False)

            def down(j, c):
                a, jj = divmod(j, ND // 2)
                tok = slice(TD * jj, TD * jj + TD)
                pe.wait_ge(s_alo, NT * a + c + 1)
                pe.wait_ge(s_wlo, w_ready(P_DN + c // 3))
                for ap_, wp in ((0, 0), (0, 1), (1, 0)):
                    last = mm(ps[0:TD, down_bank(j), 0:D], acts[:, a, c, ap_, tok], wd[:, c // 3, wp, c % 3],
                              start=False, stop=(c == NT - 1 and ap_ == 1))
                return last

            v_proj(4)
            v_proj(5)
            scores(0)
            pe.wait_ge(s_smlo, 1)
            for i in range(0, 14):
                if i < NG:
                    subtract_max(i)
                for c in {10: (8,), 12: (10,)}.get(i, ()):
                    expert(0, c)
                if 3 <= i < NG + 3:
                    h1_transpose(i - 3)
                if 2 <= i < NG + 2:
                    project(i - 2)
                for c in {8: (4,), 9: (7,)}.get(i, ()):
                    expert(0, c)
                if 3 <= i < NG + 3:
                    logits(i - 3)
                for c in {6: (0,), 7: (2,), 8: (5,)}.get(i, ()):
                    expert(0, c)
                if 1 <= i < NG + 1:
                    weighted(i - 1)
                for c in {6: (1,), 7: (3,)}.get(i, ()):
                    expert(0, c)
                if i < NG - 1:
                    scores(i + 1)
                for c in {13: (11,)}.get(i, ()):
                    expert(0, c)
                if 3 <= i < NG + 3:
                    w_transpose(i - 3)
                if i < NG:
                    p_transpose(i)
                for c in {8: (6,), 10: (9,)}.get(i, ()):
                    expert(0, c)
            for c in range(NT):
                expert(1, c)
                if c == 0:
                    pe.wait_ge(s_olo, 2 * NG)
                    for j in range(ND // 2):
                        down_bias(j)
                for j in range(ND // 2):
                    last = down(j, c)
                    if c == NT - 1:
                        last.then_inc(s_dn, 1)
            pe.wait_ge(s_g, 2 * NT)
            pe.wait_ge(s_u, 2 * NT)
            pe.wait_ge(s_wbc, 2 * NT)
            for j in range(ND // 2, ND):
                down_bias(j)
                for c in range(NT):
                    last = down(j, c)
                last.then_inc(s_dn, 1)


def kernel(x, L0_tok_W, L0_tok_b, L0_attn_w_qkv, L0_attn_w_out, L0_attn_b_out, L0_attn_scale, L0_ffn_Wr, L0_ffn_br,
           L0_ffn_Wgu, L0_ffn_bgu, L0_ffn_Wd, L0_ffn_bd):
    import numpy as np
    import concourse.bacc as bacc
    from concourse.bass_utils import run_bass_kernel_spmd

    def arr(a):
        return np.asarray(a)

    p = 16
    xT = arr(x).reshape(B, 6, p, 6, p, 3).transpose(2, 4, 5, 0, 1, 3).reshape(NC, 128, T)
    w_tok = arr(L0_tok_W).reshape(NC, 128, D)
    w_tok = np.concatenate([w_tok, w_tok[:, :, DA:]], axis=2)
    wqkvT = arr(L0_attn_w_qkv).T.reshape(D, 3, PD).transpose(1, 0, 2)
    w_outT = arr(L0_attn_w_out).T.reshape(NC, 128, D).reshape(2, 3, 128, D).transpose(0, 2, 1, 3)\
        .reshape(2, 128, 3 * D)

    def tiles(a):
        lead = a.shape[0]
        a = a.reshape(lead, NPAIR, 2, 2, FI)
        full = a[..., :DA].transpose(0, 1, 3, 2, 4).reshape(lead, NPAIR, 2, 2 * DA)
        rest = a[..., DA:].transpose(0, 1, 3, 2, 4).reshape(lead, NPAIR, 2, 2 * DB)
        return np.concatenate([full, rest], axis=3).reshape(lead, NPAIR, 6 * 128)
    w_gu = tiles(arr(L0_ffn_Wgu).transpose(1, 0, 2).reshape(D, E * 2 * FI)).transpose(1, 0, 2)
    b_gu = tiles(arr(L0_ffn_bgu).reshape(1, E * 2 * FI)).reshape(NPAIR * 6, 128).T
    wd = arr(L0_ffn_Wd).reshape(NPAIR, 2, FI, D)
    wd = np.concatenate([wd[:, :, :DA].reshape(NPAIR, 2 * DA, D), wd[:, :, DA:].reshape(NPAIR, 2 * DB, D)], axis=1)
    wd = wd.reshape(4, 3, 128, D).transpose(0, 2, 1, 3).reshape(4, 128, 3 * D)

    small = np.zeros((128, C_SMALL), np.float32)
    tok_b = arr(L0_tok_b)
    small[:, C_TOKB] = tok_b[:DA]
    small[:DB, C_TOKB + 1] = small[DB:, C_TOKB + 1] = tok_b[DA:]
    small[:, C_SCALE:C_SCALE + NP] = np.repeat(arr(L0_attn_scale).reshape(NP, 2).T, DH, axis=0)
    small[:, C_BR:C_BR + E] = arr(L0_ffn_br)
    small[:, C_BGU:C_BGU + 2 * NT] = b_gu
    small[:, C_IOTA:C_IOTA + E] = np.arange(E)
    small[BOUT_ROW, C_BD:C_BD + D] = arr(L0_attn_b_out)
    small[:, C_WR:C_WR + E] = arr(L0_ffn_Wr)[:DA]
    small[:DB, C_WR + E:C_WR + 2 * E] = small[DB:, C_WR + E:C_WR + 2 * E] = arr(L0_ffn_Wr)[DA:]
    small[0:E, C_BD:C_BD + D] = small[32:32 + E, C_BD:C_BD + D] = arr(L0_ffn_bd)

    ins = {"xT": xT, "w_tok": w_tok, "w_qkv_a": wqkvT[:, :DA], "w_qkv_b": wqkvT[:, DA:], "w_out": w_outT,
           "w_gu_a": w_gu[:, :DA], "w_gu_b": w_gu[:, DA:], "w_down": wd, "small": small}
    nc = bacc.Bacc("TRN2", target_bir_lowering=False, num_devices=1)
    arrays, aps = {}, []
    for name, a in ins.items():
        arrays[name] = np.ascontiguousarray(a)
        aps.append(nc.dram_tensor(name, a.shape, mybir.dt.float32, kind="ExternalInput").ap())
    out = nc.dram_tensor("out", (T, D), mybir.dt.float32, kind="ExternalOutput").ap()
    vit_layer(nc, *aps, out)
    r = run_bass_kernel_spmd(nc, [arrays], core_ids=[0])
    return r.results[0]["out"].reshape(B, SEQ, D)
```
